# Optimizing a Trainium2 kernel written in Bass

```python
import numpy as np
import jax
import jax.numpy as jnp

def _softmax(x, axis=-1):
    return jax.nn.softmax(x, axis=axis)

def _gelu(x):
    return jax.nn.gelu(x, approximate=True)

def _silu(x):
    return jax.nn.silu(x)

def _sigmoid(x):
    return jax.nn.sigmoid(x)

def _layernorm(x, axis=-1, eps=1e-05):
    m = jnp.mean(x, axis=axis, keepdims=True)
    v = jnp.var(x, axis=axis, keepdims=True)
    return (x - m) / jnp.sqrt(v + eps)

def _scatter_add(tgt, idx, src, axis=0):
    return tgt.at[idx].add(src)

def _segment_sum(src, seg, n):
    return jax.ops.segment_sum(src, seg, n)
kernel_name = 'mk_gnn_resnorm_d2_gnn_r8_15daa0'

def setup_inputs(seed: int=0):
    np.random.seed(seed)
    _w = jnp.asarray

    def _rec_inputs():
        import jax
        import jax.numpy as jnp
        _gk = jax.random.key(seed)
        x = -0.0002117 + 1 * jax.random.normal(jax.random.fold_in(_gk, 1), (12500, 256), jnp.float32)
        src = jax.random.randint(jax.random.fold_in(_gk, 2), (200000,), 0, 12500, jnp.int32)
        dst = jax.random.randint(jax.random.fold_in(_gk, 3), (200000,), 0, 12500, jnp.int32)
        _o = jnp.argsort(dst, stable=True)
        src = src[_o]
        dst = dst[_o]
        edge_weight = jax.random.uniform(jax.random.fold_in(_gk, 12), (200000,), jnp.float32, 0.0, 0.999998)
        return (x, src, dst, edge_weight)
    x, src, dst, edge_weight = _rec_inputs()

    def _L0_gnn_setup():
        import jax, jax.numpy as jnp
        import numpy as np
        N, D_DIM, K, R = (12500, 256, 4, 16)
        E_RAND = 200000
        ETA, LAM, C = (0.5, 0.1, 0.5)
        key = jax.random.key(seed)
        k1, k2, k3, k4 = jax.random.split(key, 4)
        Z = jax.random.normal(k1, (N, D_DIM), jnp.float32)
        U = jax.random.normal(k2, (K, D_DIM, R), jnp.float32) / np.float32(np.sqrt(D_DIM))
        Dmat = jax.random.normal(k3, (D_DIM, D_DIM), jnp.float32) / np.float32(np.sqrt(D_DIM))
        head_w = jnp.ones((K,), jnp.float32) / K
        rnd = jax.random.randint(k4, (2, E_RAND), 0, N)
        loops = jnp.stack([jnp.arange(N), jnp.arange(N)])
        edge_index = jnp.concatenate([rnd, loops], axis=1)
        return {'Z': Z, 'U': U, 'Dmat': Dmat, 'head_w': head_w, 'edge_index': edge_index}
    _L0_gnn_all = _L0_gnn_setup()
    _L0_gnn_in = {k: v for k, v in _L0_gnn_all.items() if k in ('U', 'Dmat', 'head_w')}
    del _L0_gnn_all

    def _L1_gnn_setup():
        import jax, jax.numpy as jnp
        import numpy as np
        N = 12500
        E = 37500
        D = 256

        def _mean_aggregate(x, edge_index, num_nodes):
            src, dst = (edge_index[0], edge_index[1])
            msgs = x[src]
            summed = jax.ops.segment_sum(msgs, dst, num_segments=num_nodes)
            counts = jax.ops.segment_sum(jnp.ones((edge_index.shape[1],), x.dtype), dst, num_segments=num_nodes)
            return summed / jnp.maximum(counts, 1.0)[:, None]
        key = jax.random.key(seed)
        k1, k2, k3, k4, k5, k6 = jax.random.split(key, 6)
        x = jax.random.normal(k1, (N, D), dtype=jnp.float32)
        edge_index = jax.random.randint(k2, (2, E), 0, N, dtype=jnp.int64)
        edge_weight = jax.random.uniform(k3, (E,), dtype=jnp.float32)
        lim = 1.0 / np.sqrt(D)
        W_l = jax.random.uniform(k4, (D, D), dtype=jnp.float32, minval=-lim, maxval=lim)
        b_l = jax.random.uniform(k5, (D,), dtype=jnp.float32, minval=-lim, maxval=lim)
        W_r = jax.random.uniform(k6, (D, D), dtype=jnp.float32, minval=-lim, maxval=lim)
        return {'x': x, 'edge_index': edge_index, 'edge_weight': edge_weight, 'W_l': W_l, 'b_l': b_l, 'W_r': W_r}
    _L1_gnn_all = _L1_gnn_setup()
    _L1_gnn_in = {k: v for k, v in _L1_gnn_all.items() if k in ('W_l', 'b_l', 'W_r')}
    del _L1_gnn_all
    return {'x': x, 'src': src, 'dst': dst, 'edge_weight': edge_weight, 'L0_gnn_U': _L0_gnn_in['U'], 'L0_gnn_Dmat': _L0_gnn_in['Dmat'], 'L0_gnn_head_w': _L0_gnn_in['head_w'], 'L1_gnn_W_l': _L1_gnn_in['W_l'], 'L1_gnn_b_l': _L1_gnn_in['b_l'], 'L1_gnn_W_r': _L1_gnn_in['W_r']}

def reference(x, src, dst, edge_weight, L0_gnn_U, L0_gnn_Dmat, L0_gnn_head_w, L1_gnn_W_l, L1_gnn_b_l, L1_gnn_W_r):
    import jax
    import jax.numpy as jnp

    def _L0_gnn_ref(Z, U, Dmat, head_w, edge_index):
        import jax, jax.numpy as jnp
        import numpy as np
        N, D_DIM, K, R = (12500, 256, 4, 16)
        E_RAND = 200000
        ETA, LAM, C = (0.5, 0.1, 0.5)
        src, dst = (edge_index[0], edge_index[1])
        scale = np.float32(np.sqrt(R))
        ZU = jnp.einsum('nd,kdr->knr', Z, U)
        zs = ZU[:, src, :]
        zd = ZU[:, dst, :]
        logits = (zs * zd).sum(-1) / scale
        seg_max = jax.vmap(lambda l: jax.ops.segment_max(l, dst, num_segments=N))(logits)
        exp_l = jnp.exp(logits - seg_max[:, dst])
        seg_sum = jax.vmap(lambda e: jax.ops.segment_sum(e, dst, num_segments=N))(exp_l)
        alpha = exp_l / (seg_sum[:, dst] + 1e-16)
        weighted = alpha[..., None] * zs
        agg = jax.vmap(lambda w_: jax.ops.segment_sum(w_, dst, num_segments=N))(weighted)
        w = jax.nn.softmax(head_w)
        ssa = jnp.einsum('k,knr,kdr->nd', w, agg, U)
        Z_half = (1.0 - C) * Z + C * ssa
        DZ = Z_half @ Dmat.T
        residual = Z_half - DZ @ Dmat
        grad_step = Z_half + ETA * (residual @ Dmat)
        return jax.nn.relu(grad_step - ETA * LAM)

    def _L1_gnn_ref(x, edge_index, edge_weight, W_l, b_l, W_r):
        import jax, jax.numpy as jnp
        import numpy as np
        N = 12500
        E = 37500
        D = 256

        def _mean_aggregate(x, edge_index, num_nodes):
            src, dst = (edge_index[0], edge_index[1])
            msgs = x[src]
            summed = jax.ops.segment_sum(msgs, dst, num_segments=num_nodes)
            counts = jax.ops.segment_sum(jnp.ones((edge_index.shape[1],), x.dtype), dst, num_segments=num_nodes)
            return summed / jnp.maximum(counts, 1.0)[:, None]
        h = x
        agg = _mean_aggregate(x, edge_index, x.shape[0])
        out = agg @ W_l.T + b_l
        out = out + x @ W_r.T
        out = jax.nn.relu(out)
        return out + h
    edge_index = jnp.stack([src, dst])
    x = _layernorm(x + _L0_gnn_ref(x, L0_gnn_U, L0_gnn_Dmat, L0_gnn_head_w, edge_index), axis=-1)
    x = _layernorm(x + _L1_gnn_ref(x, edge_index, edge_weight, L1_gnn_W_l, L1_gnn_b_l, L1_gnn_W_r), axis=-1)
    return x

_drawn_inputs = setup_inputs


def setup_inputs(seed=0):
    import zlib

    import numpy as np

    out = dict(_drawn_inputs(seed))
    spreads = {'L0_gnn_head_w': (0.25, 0.6)}
    factors = {'L0_gnn_U': 3.195, 'L1_gnn_b_l': 4.6}
    for name, (base, spread) in spreads.items():
        noise = np.random.default_rng([zlib.crc32(name.encode()), seed]).standard_normal(out[name].shape)
        drawn = base * np.exp(spread * noise) if base else spread * noise
        out[name] = jnp.asarray(drawn.astype(out[name].dtype))
    for name, factor in factors.items():
        out[name] = (out[name] * factor).astype(out[name].dtype)
    return out
```

```python
from contextlib import ExitStack

import concourse.bass as bass
from concourse import mybir

P = 128
ALU = mybir.AluOpType
ACT = mybir.ActivationFunctionType
AX_X = mybir.AxisListType.X
F32 = mybir.dt.float32
I32 = mybir.dt.int32
U32 = mybir.dt.uint32

ETA, LAM = 0.5, 0.1
STEP = ETA * LAM
MIX = 0.5
LOWEST = -1.0e38
OUT_OF_RANGE = float(1 << 20)


def wait(engine, semaphore, count):
    if not isinstance(count, int) or count > 0:
        engine.wait_ge(semaphore, count)


def rounds(engine, n, body):
    body(0)
    with engine.Fori(1, n) as i:
        body(i)


def gnn_kernel(nc, x, src, dst, U, Dmat, head_w, W_l, b_l, W_r, out):
    N, D = x.shape
    E, = src.shape
    H, _, R = U.shape
    F = H * R
    KD = D // P
    NB = -(-N // P)
    GB = 7
    NG = NB // GB
    GN = GB * P
    NQ = -(-GB // 2)
    PAIRS = [range(2 * q, min(2 * q + 2, GB)) for q in range(NQ)]
    NP = NB * P
    TAIL = N - (NB - 1) * P
    C = 34
    NCH = 46
    COLS = C * NCH
    EP = COLS * P
    ELAST = E - COLS * (P - 1)
    ROW = F + 2 * H
    FW = 64
    NF = E // FW
    NK = -(-NF // FW)
    FTAIL = NF - (NK - 1) * FW
    S1 = 3
    LOOK = S1 * C
    assert NG * GB == NB and NG % 2 == 0 and NCH % 2 == 0 and NG < NCH // S1 and 0 < ELAST <= COLS and NF * FW == E
    assert E <= EP and D == 2 * P

    zu_rows = nc.dram_tensor("zu_rows", (NP, F), F32, kind="Internal").ap()
    z_at_start = nc.dram_tensor("z_at_start", (EP, F), F32, kind="Internal").ap()
    rows0 = nc.dram_tensor("rows0", (EP, ROW), F32, kind="Internal").ap()
    x1 = nc.dram_tensor("x1", (NP, D), F32, kind="Internal").ap()
    rows1 = nc.dram_tensor("rows1", (EP, D), F32, kind="Internal").ap()
    own = [nc.dram_tensor(f"own{k}", (NP, D), F32, kind="Internal").ap() for k in range(2)]
    residual = [nc.dram_tensor(f"residual{k}", (NP, D), F32, kind="Internal").ap() for k in range(2)]

    with ExitStack() as ctx:
        def sb(name, shape, dt=F32):
            return ctx.enter_context(nc.sbuf_tensor("sb_" + name, shape, dt))

        def bank(name):
            return ctx.enter_context(nc.psum_tensor("ps_" + name, [P, 512], F32))

        def sem(name):
            return ctx.enter_context(nc.semaphore(name))

        def sems(name, n):
            return [sem(f"{name}{i}") for i in range(n)]

        big = sb("big", [P, S1 * C * D])
        slot1 = [big[:, s * C * D:(s + 1) * C * D].rearrange("p (c f) -> p c f", f=D) for s in range(S1)]
        at = [0]

        def in_big(words):
            at[0] += words
            assert at[0] <= S1 * C * D
            return big[:, at[0] - words:at[0]]

        regA = in_big(4 * C * F)
        found = regA[:, 0:NB * FW].bitcast(I32).rearrange("p (b j) -> p b j", j=FW)
        dst_i = regA[:, NB * FW:NB * FW + COLS + 2].bitcast(I32)
        zero = sb("zero", [P, C * F // 4])
        zs = [regA[:, s * C * F:(s + 1) * C * F].rearrange("p (c f) -> p c f", f=F) for s in range(2)]
        zd = [regA[:, (2 + s) * C * F:(3 + s) * C * F].rearrange("p (c f) -> p c f", f=F) for s in range(2)]
        zu = in_big(NB * F).rearrange("p (b f) -> p b f", f=F)
        onehot = [in_big(GN)[0:NK, :] for _ in range(2)]
        rows0_words = in_big(2 * C * ROW)
        row0 = [rows0_words[:, s * C * ROW:(s + 1) * C * ROW].rearrange("p (c f) -> p c f", f=ROW) for s in range(2)]
        col_i = rows0_words[:, 0:COLS].bitcast(I32)
        same, ends = (rows0_words[:, k * COLS:(k + 1) * COLS] for k in (1, 2))
        Wraw = in_big(2 * KD * D).rearrange("p (w k n) -> p w k n", w=2, k=KD)
        Dm = in_big(KD * D).rearrange("p (k n) -> p k n", k=KD)
        DtD = in_big(KD * D).rearrange("p (k n) -> p k n", k=KD)
        yg = [big[:, s * GB * D:(s + 1) * GB * D].rearrange("p (b f) -> p b f", f=D) for s in range(2)]
        aggn = [big[:, 2 * GB * D + s * GB * F:2 * GB * D + (s + 1) * GB * F].rearrange("p (b f) -> p b f", f=F)
                for s in range(2)]
        turned = [big[:, 2 * GB * (D + F) + q * 2 * D:2 * GB * (D + F) + (q + 1) * 2 * D].rearrange(
            "p (j f) -> p j f", f=D) for q in range(NQ)]
        at_normed = 2 * GB * (D + F) + NQ * 2 * D
        normed = [big[:, at_normed + s * GB * D:at_normed + (s + 1) * GB * D].rearrange("p (b f) -> p b f", f=D)
                  for s in range(2)]

        xg = [sb(f"xg{s}", [P, GB, D])[:, :, :] for s in range(2)]
        hg = [sb(f"hg{s}", [P, GB, D])[:, :, :] for s in range(2)]
        ng1 = [sb(f"ng{s}", [P, GB, D])[:, :, :] for s in range(2)]
        ng0 = [n.rearrange("p b f -> p (b f)")[:, 0:GB * ROW].rearrange("p (b f) -> p b f", f=ROW) for n in ng1]
        tileT = [sb(f"tileT{s}", [P, 4 * P]) for s in range(2)]

        src_i = sb("src_i", [P, COLS + LOOK], I32)
        keep = sb("keep", [P, COLS])
        scratch = sb("scratch", [P, 1536])
        ident = sb("ident", [P, P])
        shift = sb("shift", [P, P])
        wrap = sb("wrap", [P, P])
        ones_row = sb("ones_row", [1, P])
        neg_step = sb("neg_step", [P, 1])
        eps = sb("eps", [P, 1])
        node_i = sb("node_i", [P, NB], I32)
        node = sb("node", [P, NB])
        part_i = sb("part_i", [P, 1], I32)
        part = sb("part", [P, 1])
        Uc = sb("Uc", [P, KD, F])
        M = sb("M", [P, KD, D])
        G = sb("G", [F, D])
        WT = sb("WT", [P, 2, KD, D])
        bias = sb("bias", [1, D])
        hw = sb("hw", [F, 3, H])
        hws = sb("hws", [F, 4])
        fence_i = sb("fence_i", [NK, FW + 2], I32)
        fence = sb("fence", [NK, FW + 1])
        lo = sb("lo", [NK, NG])
        hi = sb("hi", [NK, NG])
        fcount = sb("fcount", [P, NB])
        fbase = sb("fbase", [P, NB])
        frow = sb("frow", [P, NB])
        frow_i = sb("frow_i", [P, NB], I32)
        first = sb("first", [P, NB + 1])
        degree = sb("degree", [P, NB])
        filled = sb("filled", [P, NB])
        inv = sb("inv", [P, NB])
        tmpn = sb("tmpn", [P, NB])
        last_i = sb("last_i", [P, NB + 2 * GB], I32)
        scat_i = sb("scat_i", [P, NB], I32)
        endf = sb("endf", [P, 4])
        end_i = sb("end_i", [P, 1], I32)
        keep_all = sb("keep_all", [P, 1])
        idx = [sb(f"idx{s}", [P, C], I32) for s in range(S1)]
        nidx = [sb(f"nidx{s}", [P, GB], I32) for s in range(2)]
        zcar = sb("zcar", [P, F])
        scar = sb("scar", [P, F + H])
        logit = sb("logit", [P, H, C])
        kneg = sb("kneg", [P, C])
        mx = [sb(f"mx{s}", [P, H, C + 1]) for s in range(2)]
        ex = sb("ex", [P, 2, H, C])
        rec = sb("rec", [P, GB, H])
        stats = [sb(f"stats{s}", [P, GB, 6]) for s in range(2)]
        mv = [sb(f"mv{s}", [P, GB, 2]) for s in range(2)]
        rstd = [sb(f"rstd{s}", [P, GB]) for s in range(2)]
        shiftm = [sb(f"shiftm{s}", [P, GB]) for s in range(2)]
        zhead = sb("zhead", [P, F])

        got = scratch[:, 0:D]

        T = [bank("T0"), bank("T1")]
        O = [bank("O0"), bank("O1")]
        B = [bank("B0"), bank("B1")]
        Q = [bank("Q0"), bank("Q1")]
        T_of = [t[:, :].rearrange("p (j f) -> p j f", f=D) for t in T + Q]
        O_of = [t[:, :].rearrange("p (j f) -> p j f", f=D) for t in O + B]

        pads_set = sem("pads_set"); zero_set = sem("zero_set"); fences_loaded = sem("fences_loaded"); edges_loaded = sem("edges_loaded")
        weights_loaded = sem("weights_loaded"); iotas_done = sem("iotas_done"); consts_done = sem("consts_done")
        zero_filled = sems("zero_filled", 2)
        ZERO_FIRST = NCH // 2 - NG
        xg_loaded = sems("xg_loaded", 2); xg_used = sems("xg_used", 2)
        xt_made = sem("xt_made"); xt_copied = sem("xt_copied"); zu_made = sem("zu_made"); zu_copied = sem("zu_copied")
        zu_stored = sem("zu_stored"); dve_step = sem("dve_step")
        hot_made = sems("hot_made", 2); hot_used = sems("hot_used", 2); picked_used = sems("picked_used", 2)
        hot_begun = sem("hot_begun"); compared = sem("compared"); counted = sem("counted")
        rows_known = sem("rows_known"); found_rows = sem("found_rows"); first_known = sem("first_known")
        next_made = sem("next_made"); nodes_known = sem("nodes_known"); z_scattered = sem("z_scattered")
        zcar_loaded = sem("zcar_loaded")
        w_pe = sem("w_pe"); w_dve = sem("w_dve"); w_exp = sem("w_exp")
        idx_ready = sems("idx_ready", 2); zs_gathered = sems("zs_gathered", 2)
        zd_loaded = sems("zd_loaded", 2); zd_used = sems("zd_used", 2)
        zd_filled = sem("zd_filled"); zcar_saved = sem("zcar_saved"); product_done = sem("product_done")
        kneg_done = sem("kneg_done"); mcar_done = sem("mcar_done"); max_done = sem("max_done")
        diff_done = sem("diff_done"); exp_done = sem("exp_done"); max_stored = sem("max_stored")
        restart_added = sem("restart_added"); weighted = sem("weighted")
        sums_done = sems("sums_done", 2); scar_saved = sem("scar_saved"); rows0_stored = sems("rows0_stored", 2)
        mend_pe = sem("mend_pe"); mend_dve = sem("mend_dve"); mend_act = sem("mend_act"); mend_dma = sem("mend_dma")
        zd_begun = sem("zd_begun"); head_made = sem("head_made"); sums_begun = sem("sums_begun")
        bg_loaded = sems("bg_loaded", 2); bg_turned = sems("bg_turned", 2); bg_copied = sems("bg_copied", 2)
        bg_made = sems("bg_made", 2); bg_out = sems("bg_out", 2); bg_done = sems("bg_done", 2)
        bg_stored = sems("bg_stored", 2)

        def slot_sems(name):
            return [sems(f"{name}{layer}_", 2) for layer in range(2)]

        n_gathered = slot_sems("n_gathered"); n_loaded = slot_sems("n_loaded"); n_stored = slot_sems("n_stored")
        agg_step = sem("agg_step"); n_idx = sems("n_idx", 2); n_scaled = sem("n_scaled"); n_turned = sems("n_turned", 2)
        n_copied = sems("n_copied", 2); n_made = sems("n_made", 2); n_taken = sems("n_taken", 2)
        n_summed = sems("n_summed", 2); n_stats = sems("n_stats", 2); n_mv = sems("n_mv", 2)
        n_std = sems("n_std", 2); n_inv = sems("n_inv", 2); n_rstd = sems("n_rstd", 2); n_normed = sems("n_normed", 2)
        idx1_ready = sems("idx1_ready", S1); r_gathered = sems("r_gathered", S1); r_scanned = sems("r_scanned", S1)
        r_stored = sems("r_stored", S1); car1_saved = sem("car1_saved"); car1_added = sem("car1_added")
        DA = 15
        NW = 9

        gate = sem("gate")

        block = ctx.enter_context(nc.Block())

        def edge_cols(dram, c):
            return dram.rearrange("(p c) f -> p c f", p=P)[:, bass.ds(c * C, C), :]

        def blocks(dram, g, first_block, n):
            return dram[bass.ds((g * GB + first_block) * P, n * P), :].rearrange("(b p) f -> p b f", p=P)

        def node_group(dram, g):
            return blocks(dram, g, 0, GB)

        @block.sync
        def _(sp):
            sp.wait_ge(pads_set, 5)
            every = dst[0:E:FW]
            with nc.allow_non_contiguous_dma(reason="one word of every 64"):
                sp.dma_start(fence_i[0:NK - 1, 0:FW], every[0:(NK - 1) * FW].rearrange("(k j) -> k j", j=FW)
                             ).then_inc(fences_loaded, 16)
                sp.dma_start(fence_i[NK - 1:NK, 0:FTAIL], every[(NK - 1) * FW:NF].rearrange("(k j) -> k j", k=1)
                             ).then_inc(fences_loaded, 16)
                sp.dma_start(fence_i[0:NK - 1, FW + 1:FW + 2],
                             dst[FW * FW:FW * FW * (NK - 1) + 1:FW * FW].rearrange("(k j) -> k j", j=1)
                             ).then_inc(fences_loaded, 16)
                whole = dst[0:COLS * (P - 1)].rearrange("(p c) -> p c", c=COLS)
                sp.dma_start(dst_i[0:P - 1, 1:COLS + 1], whole).then_inc(edges_loaded, 16)
                sp.dma_start(dst_i[P - 1:P, 1:ELAST + 1],
                             dst[COLS * (P - 1):E].rearrange("(p c) -> p c", p=1)).then_inc(edges_loaded, 16)
                sp.dma_start(dst_i[1:P, 0:1], whole[:, COLS - 1:COLS]).then_inc(edges_loaded, 16)
                sp.dma_start(dst_i[0:P - 1, COLS + 1:COLS + 2],
                             dst[COLS:COLS * (P - 1) + 1:COLS].rearrange("(p c) -> p c", c=1)
                             ).then_inc(edges_loaded, 16)
            sp.dma_start(src_i[0:P - 1, 0:COLS], src[0:COLS * (P - 1)].rearrange("(p c) -> p c", c=COLS)
                         ).then_inc(edges_loaded, 16)
            sp.dma_start(src_i[P - 1:P, 0:ELAST],
                         src[COLS * (P - 1):E].rearrange("(p c) -> p c", p=1)).then_inc(edges_loaded, 16)
            for h in range(H):
                sp.dma_start(Uc[:, :, h * R:(h + 1) * R], U[h].rearrange("(k p) r -> p k r", p=P)
                             ).then_inc(weights_loaded, 16)
            sp.dma_start(Dm[:, :, :], Dmat.rearrange("(k p) n -> p k n", p=P)).then_inc(weights_loaded, 16)
            sp.dma_start(Wraw[:, 0, :, :], W_l.rearrange("(k p) n -> p k n", p=P)).then_inc(weights_loaded, 16)
            sp.dma_start(Wraw[:, 1, :, :], W_r.rearrange("(k p) n -> p k n", p=P)).then_inc(weights_loaded, 16)
            sp.dma_start(bias[:, :], b_l.rearrange("(a n) -> a n", a=1)).then_inc(weights_loaded, 16)
            sp.dma_start(hw[:, 0, :], head_w.rearrange("(a n) -> a n", a=1).broadcast_to([F, H])
                         ).then_inc(weights_loaded, 16)

            def load_group(to, dram, g, done, rows=P):
                sp.dma_start(to[:, 0:GB - 1, :], blocks(dram, g, 0, GB - 1)).then_inc(done, 16)
                sp.dma_start(to[0:rows, GB - 1, :], dram[bass.ds((g * GB + GB - 1) * P, rows), :]
                             ).then_inc(done, 16)

            def load_x(i, s, rows=P):
                wait(sp, xg_used[s], i)
                load_group(xg[s], x, 2 * i + s, xg_loaded[s], rows)

            def store_zu(i, s):
                sp.wait_ge(zu_copied, 2 * i + s + 1)
                sp.dma_start(node_group(zu_rows, 2 * i + s), zu[:, bass.ds((2 * i + s) * GB, GB), :]
                             ).then_inc(zu_stored, 16)

            load_x(0, 0)
            load_x(0, 1)
            with sp.Fori(1, NG // 2 - 1) as i:
                for s in range(2):
                    load_x(i, s)
                for s in range(2):
                    store_zu(i - 1, s)
            load_x(NG // 2 - 1, 0)
            load_x(NG // 2 - 1, 1, rows=TAIL)
            for i in (NG // 2 - 2, NG // 2 - 1):
                for s in range(2):
                    store_zu(i, s)

            def bg_load(layer, g, rows=P):
                wait(sp, bg_done[layer], g)
                load_group(xg[0], x if layer == 0 else x1, g, bg_loaded[layer], rows)

            def bg_store(layer, g):
                sp.wait_ge(bg_done[layer], g + 1)
                sp.dma_start(node_group(own[layer], g), hg[0]).then_inc(bg_stored[layer], 16)
                sp.dma_start(node_group(residual[layer], g), hg[1]).then_inc(bg_stored[layer], 16)

            sp.wait_ge(z_scattered, 16 * NB)
            sp.wait_ge(zcar_loaded, 16)

            def load_zd(i):
                for s in range(2):
                    wait(sp, zd_used[s], i)
                    sp.dma_start(zd[s], edge_cols(z_at_start, 2 * i + s)).then_inc(zd_loaded[s], 16)

            load_zd(0)
            bg_load(0, 0)
            with sp.Fori(1, NG - 1) as i:
                load_zd(i)
                bg_store(0, i - 1)
                bg_load(0, i)
            load_zd(NG - 1)
            bg_store(0, NG - 2)
            bg_load(0, NG - 1, rows=TAIL)
            load_zd(NG)
            bg_store(0, NG - 1)
            with sp.Fori(NG + 1, NCH // 2) as i:
                load_zd(i)

            def node_in(layer, i, s):
                wait(sp, n_made[0] if layer == 0 else n_summed[1], NQ * (2 * i + s - 1))
                sp.dma_start(yg[s], node_group(own[layer], 2 * i + s)).then_inc(n_loaded[layer][s], 16)
                if layer == 0:
                    wait(sp, n_summed[0], NQ * (2 * i + s - 1))
                sp.dma_start(xg[s], node_group(residual[layer], 2 * i + s)).then_inc(n_loaded[layer][s], 16)

            def node_phase(layer):
                sp.wait_ge(bg_stored[layer], 32 * NG)
                for s in range(2):
                    node_in(layer, 0, s)
                with sp.Fori(1, NG // 2) as i:
                    for s in range(2):
                        node_in(layer, i, s)

            sp.wait_ge(mend_dve, DA)
            node_phase(0)
            for s in range(2):
                sp.wait_ge(n_stored[0][s], 32 * (NG // 2))

            def store_rows1(i, s):
                sp.wait_ge(car1_saved, S1 * i + s + 2)
                sp.dma_start(edge_cols(rows1, S1 * i + s), slot1[s]).then_inc(r_stored[s], 16)

            bg_load(1, 0)
            for s in range(S1):
                store_rows1(0, s)
            with sp.Fori(1, NG) as i:
                bg_store(1, i - 1)
                bg_load(1, i)
                for s in range(S1):
                    store_rows1(i, s)
            bg_store(1, NG - 1)
            for k in range(S1 * NG, NCH):
                store_rows1(k // S1, k % S1)
            sp.wait_ge(mend_dve, DA + 9)
            node_phase(1)
            for s in range(2):
                sp.wait_ge(n_stored[1][s], 32 * (NG // 2))

        @block.gpsimd
        def _(pool):
            pool.iota(node_i[:, :], pattern=[[P, NB]], base=0, channel_multiplier=1).then_inc(iotas_done, 1)
            pool.iota(part_i[:, :], pattern=[[0, 1]], base=0, channel_multiplier=COLS).then_inc(iotas_done, 1)
            pool.iota(scratch[:, 512:512 + GN].bitcast(I32), pattern=[[1, GN]], base=0, channel_multiplier=0
                      ).then_inc(iotas_done, 1)
            pool.iota(col_i, pattern=[[1, COLS]], base=0, channel_multiplier=0
                      ).then_inc(iotas_done, 1)
            pool.iota(fence_i[:, FW:FW + 1], pattern=[[0, 1]], base=0, channel_multiplier=FW
                      ).then_inc(iotas_done, 1)
            for m in (ident, shift, wrap):
                pool.memset(m[:, :], 0.0).then_inc(consts_done, 1)
            pool.wait_ge(consts_done, 3)
            for m, base, step in ((ident, 0, -1), (shift, -1, -1)):
                pool.affine_select(out=m[:, :], in_=m[:, :], compare_op=ALU.not_equal, fill=1.0, base=base,
                                   pattern=[[step, P]], channel_multiplier=1).then_inc(consts_done, 1)
            pool.affine_select(out=wrap[:, :], in_=wrap[:, :], compare_op=ALU.not_equal, fill=1.0, base=P - 1,
                               pattern=[[-1, P]], channel_multiplier=P).then_inc(consts_done, 1)

            def gather(to, table, index, done, limit=None):
                more = {} if limit is None else dict(bounds_check=limit, oob_is_err=False)
                pool.indirect_dma_start(to, None, table, bass.IndirectOffsetOnAxis(ap=index.bitcast(U32), axis=0),
                                        **more).then_inc(done, 16)

            pool.wait_ge(rows_known, 1)
            dst_rows = dst.rearrange("(r j) -> r j", j=FW)
            for b in range(NB):
                gather(found[:, b, :], dst_rows, frow_i[:, b:b + 1], found_rows)
            pool.wait_ge(nodes_known, 1)
            pool.wait_ge(zu_stored, 16 * NG)
            for q in range(2):
                pool.wait_ge(zero_filled[q], 16 * (NCH // 2))
            for b in range(NB):
                pool.indirect_dma_start(z_at_start, bass.IndirectOffsetOnAxis(ap=scat_i[:, b:b + 1].bitcast(U32), axis=0),
                                        zu[:, b, :], None, bounds_check=EP - 1, oob_is_err=False
                                        ).then_inc(z_scattered, 16)
            gather(zcar[:, :], zu_rows, dst_i[:, 1:2], zcar_loaded)

            pool.wait_ge(zcar_loaded, 16)
            def gather_zs(i):
                for s in range(2):
                    pool.wait_ge(idx_ready[s], i + 1)
                    wait(pool, sums_done[s], i)
                    pool.sem_inc(gate, 1)
                    for j in range(C):
                        gather(zs[s][:, j, :], zu_rows, idx[s][:, j:j + 1], zs_gathered[s])

            rounds(pool, NCH // 2, gather_zs)

            for s in range(2):
                pool.wait_ge(rows0_stored[s], 16 * (NCH // 2))
            pool.wait_ge(mend_dve, 1)
            gather(got[:, 0:ROW], rows0, end_i[:, 0:1], mend_dma, EP - 1)
            pool.wait_ge(mend_dve, DA)
            pool.indirect_dma_start(rows0, bass.IndirectOffsetOnAxis(ap=end_i[:, 0:1].bitcast(U32), axis=0),
                                    got[:, 0:ROW], None, bounds_check=EP - 1, oob_is_err=False
                                    ).then_inc(mend_dma, 16)
            pool.wait_ge(mend_dma, 32)

            def node_gathers(layer):
                def body(i):
                    for s in range(2):
                        g = 2 * i + s
                        pool.wait_ge(n_idx[layer], g + 1)
                        wait(pool, n_scaled if layer == 0 else n_turned[1], g - 1 if layer == 0 else NQ * (g - 1))
                        pool.sem_inc(gate, 1)
                        for b in range(GB):
                            to, table = (ng0, rows0) if layer == 0 else (ng1, rows1)
                            gather(to[s][:, b, :], table, nidx[s][:, b:b + 1], n_gathered[layer][s])
                rounds(pool, NG // 2, body)

            node_gathers(0)

            for s in range(2):
                pool.wait_ge(n_stored[0][s], 32 * (NG // 2))

            def gather_rows1(i, s):
                pool.wait_ge(idx1_ready[s], i + 1)
                wait(pool, r_stored[s], 16 * i)
                pool.sem_inc(gate, 1)
                for j in range(C):
                    gather(slot1[s][:, j, :], x1, idx[s][:, j:j + 1], r_gathered[s])

            rounds(pool, NCH // S1, lambda i: [gather_rows1(i, s) for s in range(S1)])
            for s in range(NCH % S1):
                gather_rows1(NCH // S1, s)

            for s in range(S1):
                pool.wait_ge(r_stored[s], 16 * (NCH // S1 + (s < NCH % S1)))
            pool.wait_ge(mend_dve, DA + 1)
            gather(got[:, :], rows1, end_i[:, 0:1], mend_dma, EP - 1)
            pool.wait_ge(mend_dve, DA + 9)
            pool.indirect_dma_start(rows1, bass.IndirectOffsetOnAxis(ap=end_i[:, 0:1].bitcast(U32), axis=0),
                                    got[:, :], None, bounds_check=EP - 1, oob_is_err=False
                                    ).then_inc(mend_dma, 16)
            pool.wait_ge(mend_dma, 64)
            node_gathers(1)

        @block.tensor
        def _(pe):
            pe.wait_ge(consts_done, 6)

            def pick(i):
                for s in range(2):
                    pe.wait_ge(hot_made[s], i + 1)
                    wait(pe, picked_used[s], i)
                    for b in range(GB):
                        mm = pe.matmul(Q[s][:, b * (FW + 1):(b + 1) * (FW + 1)], onehot[s][:, b * P:(b + 1) * P],
                                       fence[:, :], start=True, stop=True)
                    mm.then_inc(hot_used[s], 1)

            rounds(pe, NG // 2, pick)

            pe.wait_ge(weights_loaded, 16 * NW)

            def project(i):
                for n in range(2 * GB + 1):
                    if n < 2 * GB:
                        if n % GB == 0:
                            pe.wait_ge(xg_loaded[n // GB], 32 * (i + 1))
                        for k in range(KD):
                            mm = pe.transpose(T[n % 2][:, k * P:(k + 1) * P],
                                              xg[n // GB][:, n % GB, k * P:(k + 1) * P], ident[:, :])
                        mm.then_inc(xt_made, 1)
                    if n > 0:
                        m, s = n - 1, (n - 1) // GB
                        if m == 0:
                            wait(pe, zu_copied, 2 * i)
                        pe.wait_ge(xt_copied, 2 * GB * i + m + 1)
                        for k in range(KD):
                            mm = pe.matmul(B[s][:, (m % GB) * F:(m % GB + 1) * F],
                                           tileT[m % 2][:, k * P:(k + 1) * P], Uc[:, k, :],
                                           start=(k == 0), stop=(k == KD - 1))
                        if m % GB == GB - 1:
                            mm.then_inc(zu_made, 1)

            rounds(pe, NG // 2, project)

            for m in range(KD):
                for k in range(KD):
                    mm = pe.matmul(O[0][:, m * D:(m + 1) * D], Dm[:, k, m * P:(m + 1) * P], Dm[:, k, :],
                                   start=(k == 0), stop=(k == KD - 1))
            mm.then_inc(w_pe, 1)
            pe.wait_ge(w_dve, 1)
            for m in range(KD):
                for k in range(KD):
                    mm = pe.matmul(O[1][:, m * D:(m + 1) * D], DtD[:, k, m * P:(m + 1) * P], Dm[:, k, :],
                                   start=(k == 0), stop=(k == KD - 1))
            mm.then_inc(w_pe, 1)
            for w in range(2):
                if w == 1:
                    pe.wait_ge(w_dve, 2)
                for k in range(KD):
                    for m in range(KD):
                        mm = pe.transpose(O[0][:, k * D + m * P:k * D + (m + 1) * P],
                                          Wraw[:, w, m, k * P:(k + 1) * P], ident[:, :])
                mm.then_inc(w_pe, 1)
            pe.wait_ge(w_dve, 6)
            for k in range(KD):
                mm = pe.matmul(O[1][0:F, 0:D], Uc[:, k, :], M[:, k, :], start=(k == 0), stop=(k == KD - 1))
            mm.then_inc(w_pe, 1)

            pe.wait_ge(first_known, 1)
            pe.matmul(Q[0][:, 0:NB], shift[:, :], first[:, 0:NB], start=True, stop=False)
            pe.matmul(Q[0][:, 0:NB], wrap[:, :], first[:, 1:NB + 1], start=False, stop=True).then_inc(next_made, 1)

            def background(layer):
                right_of = M if layer == 0 else WT[:, 1]

                def body(g):
                    pe.wait_ge(bg_loaded[layer], 32 * (g + 1))
                    for b in range(GB + 1):
                        if b < GB:
                            wait(pe, bg_copied[layer], GB * g + max(b - 1, 0))
                            for k in range(KD):
                                mm = pe.transpose(T[b % 2][:, k * P:(k + 1) * P], xg[0][:, b, k * P:(k + 1) * P],
                                                  ident[:, :])
                            mm.then_inc(bg_turned[layer], 1)
                        if b > 0:
                            m = b - 1
                            o = O[m % 2][:, 0:D]
                            wait(pe, bg_out[layer], GB * g + max(m - 1, 0))
                            if layer == 1:
                                pe.matmul(o, ones_row[:, :], bias[:, :], start=True, stop=False)
                            pe.wait_ge(bg_copied[layer], GB * g + m + 1)
                            for k in range(KD):
                                mm = pe.matmul(o, tileT[m % 2][:, k * P:(k + 1) * P], right_of[:, k, :],
                                               start=(layer == 0 and k == 0), stop=(k == KD - 1))
                            mm.then_inc(bg_made[layer], 1)

                rounds(pe, NG, body)

            background(0)

            pe.wait_ge(mend_dve, 5)
            for k in range(4):
                mm = pe.transpose(T[0][0:F, k * P:(k + 1) * P], scratch[:, 512 + k * F:512 + (k + 1) * F], ident[:, :])
            mm.then_inc(mend_pe, 1)
            pe.wait_ge(mend_dve, 10)
            for k in range(3):
                mm = pe.transpose(T[1][:, k * F:(k + 1) * F], scratch[0:F, 1024 + k * (P + 1):1024 + k * (P + 1) + P],
                                  ident[0:F, 0:F])
            mm.then_inc(mend_pe, 1)

            def dense(layer):
                parts = 1 if layer == 0 else KD
                width = F if layer == 0 else P

                def body(i):
                    for s in range(2):
                        g = 2 * i + s
                        pe.wait_ge(n_scaled if layer == 0 else n_gathered[1][s],
                                   g + 1 if layer == 0 else 16 * GB * (i + 1))
                        for q in range(NQ + 1):
                            if q < NQ:
                                wait(pe, n_copied[layer], NQ * (g - 1) + q + 1)
                                pe.sem_inc(gate, 1)
                                of = aggn[s] if layer == 0 else ng1[s]
                                for j, b in enumerate(PAIRS[q]):
                                    for k in range(parts):
                                        mm = pe.transpose(T_of[q][0:width, j, k * P:(k + 1) * P],
                                                          of[:, b, k * width:(k + 1) * width], ident[:, :])
                                mm.then_inc(n_turned[layer], 1)
                            if q > 0:
                                m = q - 1
                                wait(pe, n_taken[layer], NQ * (g - 1) + m + 1)
                                if layer == 0 and m == 0:
                                    pe.wait_ge(n_loaded[layer][s], 32 * (i + 1))
                                pe.wait_ge(n_copied[layer], NQ * g + m + 1)
                                for j, b in enumerate(PAIRS[m]):
                                    if layer == 0:
                                        pe.matmul(O_of[m][:, j, :], ident[:, :], yg[s][:, b, :],
                                                  start=True, stop=False)
                                    for k in range(parts):
                                        mm = pe.matmul(O_of[m][:, j, :], turned[m][0:width, j, k * P:(k + 1) * P],
                                                       G[:, :] if layer == 0 else WT[:, 0, k, :],
                                                       start=(layer == 1 and k == 0), stop=(k == parts - 1))
                                mm.then_inc(n_made[layer], 1)

                rounds(pe, NG // 2, body)

            dense(0)
            background(1)

            pe.wait_ge(mend_dve, DA + 3)
            for k in range(KD):
                mm = pe.transpose(T[0][:, k * P:(k + 1) * P], scratch[:, 512 + k * P:512 + (k + 1) * P], ident[:, :])
            mm = pe.transpose(T[0][:, KD * P:(KD + 1) * P], scratch[:, 512 + KD * P:512 + (KD + 1) * P], ident[:, :])
            mm.then_inc(mend_pe, 1)
            pe.wait_ge(mend_dve, DA + 7)
            for k in range(KD):
                mm = pe.transpose(T[1][:, k * P:(k + 1) * P], scratch[:, 1024 + k * (P + 1):1024 + k * (P + 1) + P],
                                  ident[:, :])
            mm.then_inc(mend_pe, 1)

            dense(1)

        @block.scalar
        def _(act):
            z_flat = z_at_start.rearrange("(p a) f -> p (a f)", p=P)

            def fill(k, q):
                wait(act, zero_filled[q], 16 * k)
                k = 2 * k + q
                act.dma_start(z_flat[:, bass.ds(k * C * F, C * F)].rearrange("p (a c) -> p a c", a=4),
                              zero[:, :].unsqueeze(1).broadcast_to([P, 4, C * F // 4])).then_inc(zero_filled[q], 16)

            act.wait_ge(zero_set, 1)
            rounds(act, ZERO_FIRST, lambda k: [fill(k, q) for q in range(2)])

            def project(i):
                for s in range(2):
                    for b in range(GB):
                        n = s * GB + b
                        if b in (0, GB // 2):
                            fill(ZERO_FIRST + 2 * i + s, int(b > 0))
                        act.wait_ge(xt_made, 2 * GB * i + n + 1)
                        act.copy(tileT[n % 2][:, 0:KD * P], T[n % 2][:, 0:KD * P]).then_inc(xt_copied, 1)
                    act.sem_inc(xg_used[s], 1)
                    act.wait_ge(zu_made, 2 * i + s + 1)
                    act.copy(zu[:, bass.ds((2 * i + s) * GB, GB), :],
                             B[s][:, 0:GB * F].rearrange("p (b f) -> p b f", f=F)).then_inc(zu_copied, 1)

            rounds(act, NG // 2, project)

            act.wait_ge(w_dve, 8)
            act.activation(hw[:, 1, :], hw[:, 0, :], ACT.Exp, bias=hws[:, 0:1]).then_inc(w_exp, 1)

            act.wait_ge(edges_loaded, 16 * 6)
            for s in range(2):
                act.copy(idx[s][:, :], src_i[:, s * C:(s + 1) * C]).then_inc(idx_ready[s], 1)

            def background(layer, g):
                for b in range(GB + 1):
                    if b < GB:
                        act.wait_ge(bg_turned[layer], GB * g + b + 1)
                        act.copy(tileT[b % 2][:, 0:KD * P], T[b % 2][:, 0:KD * P]).then_inc(bg_copied[layer], 1)
                    if b == 0:
                        wait(act, bg_stored[layer], 32 * g)
                        whole = [t.rearrange("p b f -> p (b f)") for t in (hg[1], xg[0])]
                        if layer == 0:
                            act.activation(whole[0], whole[1], ACT.Identity, bias=neg_step[:, 0:1])
                        else:
                            act.mul(whole[0], whole[1], 2.0)
                    else:
                        act.wait_ge(bg_made[layer], GB * g + b)
                        act.copy(hg[0][:, b - 1, :], O[(b - 1) % 2][:, 0:D]).then_inc(bg_out[layer], 1)
                act.wait_ge(bg_out[layer], GB * (g + 1))
                act.sem_inc(bg_done[layer], 1)

            def weights_of_edges(i, with_background):
                for s in range(2):
                    act.wait_ge(diff_done, 2 * (2 * i + s + 1))
                    act.activation(ex[:, :, :, :].rearrange("p a h c -> p (a h c)"),
                                   ex[:, :, :, :].rearrange("p a h c -> p (a h c)"), ACT.Exp,
                                   scale=1.0 / float(R) ** 0.5).then_inc(exp_done, 1)
                    wait(act, rows0_stored[s], 16 * i)
                    act.copy(row0[s][:, :, F + H:ROW], mx[s][:, :, 1:C + 1].rearrange("p h c -> p c h")
                             ).then_inc(max_stored, 1)
                    act.wait_ge(sums_done[s], i + 1)
                    act.wait_ge(max_stored, 2 * i + s + 1)
                    act.dma_start(edge_cols(rows0, 2 * i + s), row0[s]).then_inc(rows0_stored[s], 16)
                    act.wait_ge(zs_gathered[s], 16 * C * (i + 1))
                    act.copy(idx[s][:, :], src_i[:, bass.ds((2 * i + s + 2) * C, C)]).then_inc(idx_ready[s], 1)
                    if with_background and s == 0:
                        background(0, i)

            weights_of_edges(0, True)
            with act.Fori(1, NG) as i:
                weights_of_edges(i, True)
            with act.Fori(NG, NCH // 2) as i:
                weights_of_edges(i, False)

            scale = 1.0 / float(R) ** 0.5
            act.wait_ge(mend_dve, 8)
            act.activation(scratch[0:F, 512:512 + 2 * P], scratch[0:F, 512:512 + 2 * P], ACT.Exp, scale=scale
                           ).then_inc(mend_act, 1)
            act.wait_ge(mend_dve, 13)
            act.activation(scratch[:, 512:512 + 2 * F], scratch[:, 512:512 + 2 * F], ACT.Exp, scale=scale
                           ).then_inc(mend_act, 1)

            def node_groups(layer):
                width, part = (P, F) if layer == 0 else (KD * P, P)

                def std(i, s):
                    act.wait_ge(n_mv[layer], GB * (2 * i + s + 1))
                    act.activation(rstd[s][:, :], mv[s][:, :, 1], ACT.Sqrt, bias=eps[:, 0:1]
                                   ).then_inc(n_std[layer], 1)

                def norm(i, s, b):
                    if b == 0:
                        act.wait_ge(n_rstd[layer], 2 * i + s + 1)
                        wait(act, n_stored[layer][s], 32 * i)
                    done = act.activation(normed[s][:, b, :], hg[s][:, b, :], ACT.Identity, bias=shiftm[s][:, b:b + 1],
                                          scale=rstd[s][:, b:b + 1])
                    if b == GB - 1:
                        done.then_inc(n_normed[layer], 1)

                def store(i, s, rows=P):
                    g = 2 * i + s
                    dram = x1 if layer == 0 else out
                    act.wait_ge(n_normed[layer], g + 1)
                    act.dma_start(blocks(dram, g, 0, GB - 1), normed[s][:, 0:GB - 1, :]).then_inc(n_stored[layer][s], 16)
                    act.dma_start(dram[bass.ds((g * GB + GB - 1) * P, rows), :], normed[s][0:rows, GB - 1, :]
                                  ).then_inc(n_stored[layer][s], 16)

                def body(i):
                    for s in range(2):
                        g = 2 * i + s
                        there = not isinstance(i, int) or i > 0
                        if there:
                            std(i - 1, s)
                        for q in range(NQ):
                            act.wait_ge(n_turned[layer], NQ * g + q + 1)
                            wait(act, n_made[layer], NQ * (g - 1) + q + 1)
                            n = len(PAIRS[q])
                            act.copy(turned[q][0:part, 0:n, 0:width], T_of[q][0:part, 0:n, 0:width]
                                     ).then_inc(n_copied[layer], 1)
                            if there and q > 0:
                                for b in PAIRS[q - 1]:
                                    norm(i - 1, s, b)
                        if there:
                            norm(i - 1, s, GB - 1)
                            store(i - 1, s)

                rounds(act, NG // 2, body)
                for s in range(2):
                    std(NG // 2 - 1, s)
                    for b in range(GB):
                        norm(NG // 2 - 1, s, b)
                    store(NG // 2 - 1, s, rows=P if layer == 0 or s == 0 else TAIL)

            node_groups(0)
            rounds(act, NG, lambda g: background(1, g))
            node_groups(1)

        @block.vector
        def _(dve):
            steps = [0]

            def done(ins, which=dve_step):
                steps[0] += 1
                ins.then_inc(dve_step, 1)
                dve.wait_ge(dve_step, steps[0])

            dve.memset(zero[:, :], 0.0).then_inc(zero_set, 1)
            dve.memset(dst_i[:, 1:COLS + 2], N).then_inc(pads_set, 1)
            dve.memset(dst_i[:, 0:1], -1).then_inc(pads_set, 1)
            dve.memset(src_i[:, :], 0).then_inc(pads_set, 1)
            dve.memset(fence_i[:, 0:FW], 1 << 20).then_inc(pads_set, 1)
            dve.memset(fence_i[:, FW + 1:FW + 2], 1 << 20).then_inc(pads_set, 1)
            dve.memset(last_i[:, NB:NB + 2 * GB], 0)
            dve.memset(neg_step[:, :], -ETA * LAM)
            dve.memset(eps[:, :], 1e-5)
            dve.memset(ones_row[:, :], 1.0)
            dve.memset(first[:, NB:NB + 1], float(E))
            dve.wait_ge(iotas_done, 5)
            dve.tensor_copy(node[:, :], node_i[:, :])
            dve.tensor_copy(part[:, :], part_i[:, :])
            count = scratch[:, 512:512 + GN].bitcast(I32)

            dve.wait_ge(fences_loaded, 48)
            dve.tensor_copy(fence[:, :], fence_i[:, 0:FW + 1])
            done(dve.tensor_copy(hi[:, 0:1], fence_i[:, FW + 1:FW + 2]))
            done(dve.tensor_copy(lo[:, 0:1], fence[:, 0:1]))
            done(dve.memset(lo[0:1, 0:1], -1.0))
            for g in range(1, NG):
                dve.tensor_scalar(lo[:, g:g + 1], lo[:, 0:1], float(-g * GN), None, ALU.add)
                ins = dve.tensor_scalar(hi[:, g:g + 1], hi[:, 0:1], float(-g * GN), None, ALU.add)
            done(ins)

            def make_hot(i, s):
                g = 2 * i + s
                wait(dve, hot_used[s], i)
                dve.tensor_scalar(onehot[s], count[0:NK, :], hi[:, bass.ds(g, 1)], None, ALU.is_gt
                                  ).then_inc(hot_begun, 1)
                dve.wait_ge(hot_begun, g + 1)
                dve.scalar_tensor_tensor(out=onehot[s], in0=count[0:NK, :], scalar=lo[:, bass.ds(g, 1)],
                                         in1=onehot[s], op0=ALU.is_gt, op1=ALU.subtract).then_inc(hot_made[s], 1)

            def count_fences(i, s):
                g = 2 * i + s
                dve.wait_ge(hot_used[s], i + 1)
                q = Q[s][:, 0:GB * (FW + 1)].rearrange("p (b j) -> p b j", j=FW + 1)
                less = scratch[:, 0:GB * FW].rearrange("p (b j) -> p b j", j=FW)
                who = node[:, bass.ds(g * GB, GB)].unsqueeze(2).broadcast_to([P, GB, FW])
                wait(dve, counted, g)
                dve.tensor_tensor(less, q[:, :, 0:FW], who, ALU.is_lt).then_inc(compared, 1)
                dve.tensor_copy(fbase[:, bass.ds(g * GB, GB)], q[:, :, FW]).then_inc(picked_used[s], 1)
                dve.wait_ge(compared, g + 1)
                dve.tensor_reduce(fcount[:, bass.ds(g * GB, GB)], less, AX_X, ALU.add).then_inc(counted, 1)

            make_hot(0, 0)
            make_hot(0, 1)
            count_fences(0, 0)
            with dve.Fori(1, NG // 2) as i:
                make_hot(i, 0)
                count_fences(i - 1, 1)
                make_hot(i, 1)
                count_fences(i, 0)
            count_fences(NG // 2 - 1, 1)
            dve.wait_ge(counted, NG)
            for s in range(2):
                dve.wait_ge(picked_used[s], NG // 2)
            done(dve.scalar_tensor_tensor(out=frow[:, :], in0=fcount[:, :], scalar=-1.0, in1=fbase[:, :],
                                          op0=ALU.add, op1=ALU.add))
            done(dve.tensor_scalar(frow[:, :], frow[:, :], 0.0, None, ALU.max))
            dve.tensor_copy(frow_i[:, :], frow[:, :]).then_inc(rows_known, 1)

            dve.wait_ge(edges_loaded, 16 * 6)
            dve.tensor_tensor(keep[:, :], dst_i[:, 1:COLS + 1], dst_i[:, 0:COLS], ALU.is_equal)
            dve.tensor_copy(ends, col_i)
            done(dve.tensor_tensor(same, dst_i[:, 1:COLS + 1], dst_i[:, 2:COLS + 2], ALU.is_equal))
            done(dve.scalar_tensor_tensor(out=ends, in0=same, scalar=OUT_OF_RANGE, in1=ends, op0=ALU.mult,
                                          op1=ALU.add))
            dve.tensor_reduce(keep_all[:, :], keep[:, :], AX_X, ALU.min)
            done(dve.tensor_reduce(endf[:, 0:1], ends, AX_X, ALU.min))
            done(dve.tensor_scalar(endf[:, 1:2], keep[:, 0:1], -1.0, -OUT_OF_RANGE, ALU.add, ALU.mult))
            done(dve.scalar_tensor_tensor(out=endf[:, 2:3], in0=endf[:, 0:1], scalar=part[:, 0:1], in1=endf[:, 1:2],
                                          op0=ALU.add, op1=ALU.add))
            done(dve.tensor_copy(end_i[:, :], endf[:, 2:3]))

            dve.wait_ge(weights_loaded, 16 * NW)
            dve.wait_ge(w_pe, 1)
            dve.tensor_copy(DtD[:, :, :].rearrange("p k n -> p (k n)"), O[0][:, :]).then_inc(w_dve, 1)
            for w in range(2):
                dve.wait_ge(w_pe, 3 + w)
                dve.tensor_copy(WT[:, w, :, :].rearrange("p k n -> p (k n)"), O[0][:, :]).then_inc(w_dve, 1)
            done(dve.scalar_tensor_tensor(out=M[:, :, :].rearrange("p k n -> p (k n)"), in0=O[1][:, :], scalar=-1.0,
                                          in1=Dm[:, :, :].rearrange("p k n -> p (k n)"), op0=ALU.mult, op1=ALU.add))
            done(dve.tensor_scalar(M[:, :, :].rearrange("p k n -> p (k n)"), M[:, :, :].rearrange("p k n -> p (k n)"),
                                   MIX * ETA, None, ALU.mult))
            dve.wait_ge(consts_done, 6)
            for k in range(KD):
                dve.scalar_tensor_tensor(out=M[:, k, k * P:(k + 1) * P], in0=ident[:, :], scalar=MIX,
                                         in1=M[:, k, k * P:(k + 1) * P], op0=ALU.mult, op1=ALU.add
                                         ).then_inc(w_dve, 1)
            dve.tensor_scalar(hws[:, 1:2], part[0:F, :], 1.0 / COLS, None, ALU.mult).then_inc(w_dve, 1)
            dve.wait_ge(w_dve, 6)
            done(dve.tensor_reduce(hws[:, 2:3], hw[:, 0, :], AX_X, ALU.max))
            done(dve.tensor_scalar(hws[:, 0:1], hws[:, 2:3], -1.0, None, ALU.mult))
            for h in range(H):
                ins = dve.tensor_scalar(hw[:, 2, h:h + 1], hws[:, 1:2], float(h * R) - 0.5, None, ALU.is_gt)
            done(ins)
            dve.sem_inc(w_dve, 2)
            done(dve.tensor_tensor(hw[:, 2, 0:H - 1], hw[:, 2, 0:H - 1], hw[:, 2, 1:H], ALU.subtract))
            dve.wait_ge(w_exp, 1)
            dve.tensor_reduce(hws[:, 2:3], hw[:, 1, :], AX_X, ALU.add)
            done(dve.tensor_tensor(hw[:, 0, :], hw[:, 1, :], hw[:, 2, :], ALU.mult))
            done(dve.tensor_reduce(hws[:, 3:4], hw[:, 0, :], AX_X, ALU.add))
            done(dve.reciprocal(hws[:, 2:3], hws[:, 2:3]))
            done(dve.tensor_tensor(hws[:, 3:4], hws[:, 3:4], hws[:, 2:3], ALU.mult))
            dve.wait_ge(w_pe, 5)
            dve.tensor_scalar(G[0:F, :], O[1][0:F, 0:D], hws[:, 3:4], None, ALU.mult).then_inc(w_dve, 1)

            dve.wait_ge(found_rows, 16 * NB)
            for g in range(NG):
                less = scratch[:, 0:GB * FW].rearrange("p (b j) -> p b j", j=FW)
                who = node[:, g * GB:(g + 1) * GB].unsqueeze(2).broadcast_to([P, GB, FW])
                done(dve.tensor_tensor(less, found[:, g * GB:(g + 1) * GB, :], who, ALU.is_lt))
                done(dve.tensor_reduce(fcount[:, g * GB:(g + 1) * GB], less, AX_X, ALU.add))
            dve.scalar_tensor_tensor(out=first[:, 0:NB], in0=frow[:, :], scalar=float(FW), in1=fcount[:, :],
                                     op0=ALU.mult, op1=ALU.add).then_inc(first_known, 1)
            dve.wait_ge(next_made, 1)
            done(dve.tensor_tensor(degree[:, :], Q[0][:, 0:NB], first[:, 0:NB], ALU.subtract))
            dve.tensor_scalar(filled[:, :], degree[:, :], 0.0, None, ALU.is_gt)
            dve.tensor_scalar(last_i[:, 0:NB], Q[0][:, 0:NB], -1.0, 0.0, ALU.add, ALU.max)
            done(dve.tensor_scalar(inv[:, :], degree[:, :], 1.0, None, ALU.max))
            dve.tensor_scalar(tmpn[:, :], filled[:, :], -1.0, -OUT_OF_RANGE, ALU.add, ALU.mult)
            done(dve.reciprocal(inv[:, :], inv[:, :]))
            dve.tensor_tensor(inv[:, :], inv[:, :], filled[:, :], ALU.mult)
            dve.tensor_tensor(scat_i[:, :], first[:, 0:NB], tmpn[:, :], ALU.add).then_inc(nodes_known, 1)

            dve.memset(scar[:, :], 0.0)
            done(dve.memset(mx[1][:, :, C:C + 1], LOWEST))
            dve.wait_ge(zcar_loaded, 16)

            def edge_chunks(i):
                for s in range(2):
                    c = 2 * i + s
                    kp = keep[:, bass.ds(c * C, C)]
                    kp0 = keep[:, bass.ds(c * C, 1)]
                    dve.wait_ge(zd_loaded[s], 16 * (i + 1))
                    wait(dve, zcar_saved, c)
                    dve.scalar_tensor_tensor(out=zd[s][:, 0, :], in0=zcar[:, :], scalar=kp0, in1=zd[s][:, 0, :],
                                             op0=ALU.mult, op1=ALU.add).then_inc(zd_begun, 1)
                    dve.tensor_scalar(kneg[:, :], kp, -1.0, -LOWEST, ALU.add, ALU.mult).then_inc(kneg_done, 1)
                    dve.tensor_copy(mx[s][:, :, 0:1], mx[1 - s][:, :, C:C + 1]).then_inc(mcar_done, 1)
                    dve.wait_ge(zd_begun, c + 1)
                    for f in range(F):
                        ins = dve.tensor_tensor_scan(zd[s][:, :, f], kp, zd[s][:, :, f], 0.0, ALU.mult, ALU.add)
                    ins.then_inc(zd_filled, 1)
                    dve.wait_ge(zd_filled, c + 1)
                    dve.tensor_copy(zcar[:, :], zd[s][:, C - 1, :]).then_inc(zcar_saved, 1)
                    dve.wait_ge(zcar_saved, c + 1)
                    dve.wait_ge(zs_gathered[s], 16 * C * (i + 1))
                    dve.tensor_tensor(zd[s], zd[s], zs[s], ALU.mult).then_inc(product_done, 1)
                    dve.wait_ge(product_done, c + 1)
                    dve.tensor_reduce(logit[:, :, :].rearrange("p h c -> p c h"),
                                      zd[s].rearrange("p c (h r) -> p c h r", r=R), AX_X, ALU.add
                                      ).then_inc(zd_used[s], 1)
                    dve.wait_ge(zd_used[s], i + 1)
                    dve.wait_ge(kneg_done, c + 1)
                    dve.wait_ge(mcar_done, c + 1)
                    wait(dve, max_stored, c)
                    for h in range(H):
                        ins = dve.tensor_tensor_scan(mx[s][:, h, 1:C + 1], kneg[:, :], logit[:, h, :],
                                                     mx[s][:, h, 0:1], ALU.add, ALU.max)
                    ins.then_inc(max_done, 1)
                    dve.wait_ge(max_done, c + 1)
                    dve.tensor_tensor(ex[:, 0, :, :], mx[s][:, :, 0:C], kneg[:, :].unsqueeze(1).broadcast_to([P, H, C]),
                                      ALU.add).then_inc(restart_added, 1)
                    dve.tensor_tensor(ex[:, 1, :, :], logit[:, :, :], mx[s][:, :, 1:C + 1], ALU.subtract
                                      ).then_inc(diff_done, 1)
                    dve.wait_ge(restart_added, c + 1)
                    dve.tensor_tensor(ex[:, 0, :, :], ex[:, 0, :, :], mx[s][:, :, 1:C + 1], ALU.subtract
                                      ).then_inc(diff_done, 1)
                    dve.wait_ge(exp_done, c + 1)
                    wide = ex[:, 1, :, :].rearrange("p h c -> p c h").unsqueeze(3).broadcast_to([P, C, H, R])
                    zs4 = zs[s].rearrange("p c (h r) -> p c h r", r=R)
                    dve.tensor_tensor(zs4, zs4, wide, ALU.mult).then_inc(weighted, 1)
                    wait(dve, scar_saved, c)
                    dve.tensor_tensor(zhead[:, :].rearrange("p (h r) -> p h r", r=R),
                                      scar[:, 0:F].rearrange("p (h r) -> p h r", r=R),
                                      ex[:, 0, :, 0:1].broadcast_to([P, H, R]), ALU.mult).then_inc(head_made, 1)
                    wait(dve, rows0_stored[s], 16 * i)
                    for h in range(H):
                        dve.tensor_tensor_scan(row0[s][:, :, F + h], ex[:, 0, h, :], ex[:, 1, h, :],
                                               scar[:, F + h:F + h + 1], ALU.mult, ALU.add)
                    dve.wait_ge(weighted, c + 1)
                    dve.wait_ge(head_made, c + 1)
                    dve.tensor_tensor(zs[s][:, 0, :], zs[s][:, 0, :], zhead[:, :], ALU.add).then_inc(sums_begun, 1)
                    dve.wait_ge(sums_begun, c + 1)
                    for f in range(F):
                        ins = dve.tensor_tensor_scan(row0[s][:, :, f], ex[:, 0, f // R, :], zs[s][:, :, f],
                                                     0.0, ALU.mult, ALU.add)
                    ins.then_inc(sums_done[s], 1)
                    dve.wait_ge(sums_done[s], i + 1)
                    dve.tensor_copy(scar[:, :], row0[s][:, C - 1, 0:F + H]).then_inc(scar_saved, 1)

            rounds(dve, NCH // 2, edge_chunks)

            m = [0]

            def mend(ins):
                m[0] += 1
                ins.then_inc(mend_dve, 1)
                dve.wait_ge(mend_dve, m[0])

            lastrow = row0[1][:, C - 1, :]
            wideS = scratch[:, 512:512 + 4 * F].rearrange("p (k f) -> p k f", f=F)
            mend(dve.memset(got[:, :], 0.0))
            dve.wait_ge(scar_saved, NCH)
            dve.wait_ge(max_stored, NCH)

            def over_heads(ap):
                return ap.unsqueeze(2).broadcast_to([P, H, R])

            mend(dve.tensor_copy(wideS[:, 0, :], lastrow[:, 0:F]))
            mend(dve.tensor_copy(wideS[:, 1, :].rearrange("p (h r) -> p h r", r=R), over_heads(lastrow[:, F:F + H])))
            mend(dve.tensor_copy(wideS[:, 2, :].rearrange("p (h r) -> p h r", r=R), over_heads(lastrow[:, F + H:ROW])))
            mend(dve.tensor_copy(wideS[:, 3, :], keep_all[:, 0:1].broadcast_to([P, F])))
            dve.wait_ge(mend_pe, 1)
            tr = T[0][0:F, :].rearrange("f (k p) -> f k p", p=P)
            carry = scratch[0:F, 1024:1024 + 3 * (P + 1)].rearrange("f (k p) -> f k p", p=P + 1)
            negk = scratch[0:F, 512:512 + P]
            dve.memset(carry[:, 0:2, 0:1], 0.0)
            dve.memset(carry[:, 2, 0:1], LOWEST)
            mend(dve.tensor_scalar(negk, tr[:, 3, :], -1.0, -LOWEST, ALU.add, ALU.mult))
            mend(dve.tensor_tensor_scan(carry[:, 2, 1:P + 1], negk, tr[:, 2, :], LOWEST, ALU.add, ALU.max))
            done(dve.tensor_tensor(negk, carry[:, 2, 0:P], negk, ALU.add))
            dve.tensor_tensor(negk, negk, carry[:, 2, 1:P + 1], ALU.subtract)
            mend(dve.tensor_tensor(scratch[0:F, 512 + P:512 + 2 * P], tr[:, 2, :], carry[:, 2, 1:P + 1],
                                   ALU.subtract))
            dve.wait_ge(mend_act, 1)
            both = scratch[0:F, 512 + 2 * P:512 + 4 * P].rearrange("f (k p) -> f k p", p=P)
            mend(dve.tensor_tensor(both, tr[:, 0:2, :],
                                   scratch[0:F, 512 + P:512 + 2 * P].unsqueeze(1).broadcast_to([F, 2, P]), ALU.mult))
            dve.tensor_tensor_scan(carry[:, 0, 1:P + 1], scratch[0:F, 512:512 + P], both[:, 0, :], 0.0,
                                   ALU.mult, ALU.add)
            mend(dve.tensor_tensor_scan(carry[:, 1, 1:P + 1], scratch[0:F, 512:512 + P], both[:, 1, :], 0.0,
                                        ALU.mult, ALU.add))
            dve.wait_ge(mend_pe, 2)
            dve.wait_ge(mend_dma, 16)
            cr = T[1][:, 0:3 * F].rearrange("p (k f) -> p k f", f=F)
            wideR = scratch[:, 512 + 3 * F:512 + 6 * F].rearrange("p (k f) -> p k f", f=F)
            dve.tensor_copy(wideR[:, 0, :].rearrange("p (h r) -> p h r", r=R), over_heads(got[:, F:F + H]))
            mend(dve.tensor_copy(wideR[:, 1, :].rearrange("p (h r) -> p h r", r=R), over_heads(got[:, F + H:ROW])))
            mend(dve.tensor_tensor(wideR[:, 2, :], cr[:, 2, :], wideR[:, 1, :], ALU.max))
            dve.tensor_tensor(scratch[:, 512:512 + F], cr[:, 2, :], wideR[:, 2, :], ALU.subtract)
            mend(dve.tensor_tensor(scratch[:, 512 + F:512 + 2 * F], wideR[:, 1, :], wideR[:, 2, :], ALU.subtract))
            dve.wait_ge(mend_act, 2)
            ea = scratch[:, 512:512 + F]
            eb = scratch[:, 512 + F:512 + 2 * F]
            part1 = scratch[:, 512 + 6 * F:512 + 7 * F]
            part2 = scratch[:, 512 + 7 * F:512 + 8 * F]
            dve.tensor_tensor(part1, cr[:, 0, :], ea, ALU.mult)
            dve.tensor_tensor(part2, cr[:, 1, :], ea, ALU.mult)
            dve.tensor_tensor(got[:, 0:F], got[:, 0:F], eb, ALU.mult)
            done(dve.tensor_tensor(wideR[:, 0, :], wideR[:, 0, :], eb, ALU.mult))
            heads = [w.rearrange("p (h r) -> p h r", r=R)[:, :, 0] for w in (part2, wideR[:, 0, :], wideR[:, 2, :])]
            mend(dve.tensor_tensor(got[:, 0:F], got[:, 0:F], part1, ALU.add))
            dve.tensor_tensor(got[:, F:F + H], heads[0], heads[1], ALU.add)
            mend(dve.tensor_copy(got[:, F + H:ROW], heads[2]))
            assert m[0] == DA, m[0]

            def first_indices(layer):
                for s in range(2):
                    dve.tensor_copy(nidx[s][:, :], last_i[:, s * GB:(s + 1) * GB]).then_inc(n_idx[layer], 1)

            def next_indices(layer, i, s):
                dve.wait_ge(n_gathered[layer][s], 16 * GB * (i + 1))
                dve.tensor_copy(nidx[s][:, :], last_i[:, bass.ds((2 * i + s + 2) * GB, GB)]
                                ).then_inc(n_idx[layer], 1)

            def scale(i, s):
                g = 2 * i + s
                next_indices(0, i, s)
                wait(dve, n_scaled, g)
                dve.tensor_scalar(rec[:, :, :], ng0[s][:, :, F:F + H], 1e-16, None, ALU.add).then_inc(agg_step, 1)
                dve.wait_ge(agg_step, 3 * g + 1)
                dve.reciprocal(rec[:, :, :], rec[:, :, :]).then_inc(agg_step, 1)
                dve.wait_ge(agg_step, 3 * g + 2)
                dve.tensor_tensor(rec[:, :, :], rec[:, :, :],
                                  filled[:, bass.ds(g * GB, GB)].unsqueeze(2).broadcast_to([P, GB, H]), ALU.mult
                                  ).then_inc(agg_step, 1)
                dve.wait_ge(agg_step, 3 * g + 3)
                wait(dve, n_turned[0], NQ * (g - 1))
                dve.tensor_tensor(aggn[s].rearrange("p b (h r) -> p b h r", r=R),
                                  ng0[s][:, :, 0:F].rearrange("p b (h r) -> p b h r", r=R),
                                  rec[:, :, :].unsqueeze(3).broadcast_to([P, GB, H, R]), ALU.mult
                                  ).then_inc(n_scaled, 1)

            def finish_stats(layer, i, s):
                dve.wait_ge(n_std[layer], 2 * i + s + 1)
                dve.reciprocal(rstd[s][:, :], rstd[s][:, :]).then_inc(n_inv[layer], 1)
                dve.wait_ge(n_inv[layer], 2 * i + s + 1)
                dve.scalar_tensor_tensor(out=shiftm[s][:, :], in0=mv[s][:, :, 0], scalar=-1.0, in1=rstd[s][:, :],
                                         op0=ALU.mult, op1=ALU.mult).then_inc(n_rstd[layer], 1)

            def combine(layer, i, s):
                g = 2 * i + s
                before = (i, 0) if s else (i - 1, 1)
                there = not (isinstance(i, int) and i == 0 and s == 0)
                dve.wait_ge(n_loaded[layer][s], 32 * (i + 1))
                wait(dve, n_normed[layer], g - 1)
                for q in range(NQ + 1):
                    if q < NQ:
                        dve.wait_ge(n_made[layer], NQ * g + q + 1)
                        pair = slice(2 * q, 2 * q + len(PAIRS[q]))
                        if layer == 0:
                            dve.scalar_tensor_tensor(out=hg[s][:, pair, :], in0=O_of[q][:, 0:len(PAIRS[q]), :],
                                                     scalar=STEP, in1=xg[s][:, pair, :], op0=ALU.max, op1=ALU.add
                                                     ).then_inc(n_taken[0], 1)
                        else:
                            for j, b in enumerate(PAIRS[q]):
                                ins = dve.scalar_tensor_tensor(out=yg[s][:, b, :], in0=O_of[q][:, j, :],
                                                               scalar=inv[:, bass.ds(g * GB + b, 1)],
                                                               in1=yg[s][:, b, :], op0=ALU.mult, op1=ALU.add)
                            ins.then_inc(n_taken[1], 1)
                            dve.wait_ge(n_taken[1], NQ * g + q + 1)
                            dve.scalar_tensor_tensor(out=hg[s][:, pair, :], in0=yg[s][:, pair, :], scalar=0.0,
                                                     in1=xg[s][:, pair, :], op0=ALU.max, op1=ALU.add
                                                     ).then_inc(n_summed[1], 1)
                    if q == 1 and there:
                        finish_stats(layer, *before)
                    if q > 0:
                        dve.wait_ge(n_taken[0] if layer == 0 else n_summed[1], NQ * g + q)
                        for b in PAIRS[q - 1]:
                            dve.bn_stats(stats[s][:, b, :], hg[s][:, b, :]).then_inc(n_stats[layer], 1)
                dve.wait_ge(n_stats[layer], GB * (g + 1))
                if layer == 0:
                    dve.sem_inc(n_summed[0], NQ)
                else:
                    dve.sem_inc(gate, 1)
                for b in range(GB):
                    dve.bn_aggr(mv[s][:, b, :], stats[s][:, b, :]).then_inc(n_mv[layer], 1)

            first_indices(0)
            scale(0, 0)
            scale(0, 1)
            combine(0, 0, 0)
            with dve.Fori(1, NG // 2) as i:
                scale(i, 0)
                combine(0, i - 1, 1)
                scale(i, 1)
                combine(0, i, 0)
            combine(0, NG // 2 - 1, 1)
            finish_stats(0, NG // 2 - 1, 1)

            car = scratch[:, 512:512 + D]
            dve.memset(car, 0.0).then_inc(car1_saved, 1)
            for s in range(S1):
                dve.tensor_copy(idx[s][:, :], src_i[:, s * C:(s + 1) * C]).then_inc(idx1_ready[s], 1)

            def scan_rows(i, s):
                c = S1 * i + s
                kp = keep[:, bass.ds(c * C, C)]
                dve.wait_ge(r_gathered[s], 16 * C * (i + 1))
                dve.wait_ge(car1_saved, c + 1)
                dve.scalar_tensor_tensor(out=slot1[s][:, 0, :], in0=car, scalar=keep[:, bass.ds(c * C, 1)],
                                         in1=slot1[s][:, 0, :], op0=ALU.mult, op1=ALU.add).then_inc(car1_added, 1)
                dve.tensor_copy(idx[s][:, :], src_i[:, bass.ds((c + S1) * C, C)]).then_inc(idx1_ready[s], 1)
                dve.wait_ge(car1_added, c + 1)
                for f in range(D):
                    ins = dve.tensor_tensor_scan(slot1[s][:, :, f], kp, slot1[s][:, :, f], 0.0, ALU.mult, ALU.add)
                ins.then_inc(r_scanned[s], 1)
                dve.wait_ge(r_scanned[s], i + 1)
                dve.tensor_copy(car, slot1[s][:, C - 1, :]).then_inc(car1_saved, 1)

            rounds(dve, NCH // S1, lambda i: [scan_rows(i, s) for s in range(S1)])
            for s in range(NCH % S1):
                scan_rows(NCH // S1, s)

            mend(dve.memset(got[:, :], 0.0))
            dve.wait_ge(car1_saved, NCH + 1)
            mend(dve.tensor_copy(scratch[:, 512 + D:512 + D + P], keep_all[:, 0:1].broadcast_to([P, P])))
            carry1 = scratch[:, 1024:1024 + 2 * (P + 1)].rearrange("f (k p) -> f k p", p=P + 1)
            mend(dve.memset(carry1[:, :, 0:1], 0.0))
            dve.wait_ge(mend_pe, 3)
            keepT = scratch[:, 512 + D + P:512 + D + 2 * P]
            mend(dve.tensor_copy(keepT, T[0][:, KD * P:(KD + 1) * P]))
            for k in range(KD):
                mend(dve.tensor_tensor_scan(carry1[:, k, 1:P + 1], keepT, T[0][:, k * P:(k + 1) * P], 0.0,
                                            ALU.mult, ALU.add))
            dve.sem_inc(mend_dve, 1)
            m[0] += 1
            dve.wait_ge(mend_pe, 4)
            dve.wait_ge(mend_dma, 48)
            mend(dve.tensor_tensor(got[:, :], got[:, :], T[1][:, 0:D], ALU.add))
            dve.sem_inc(mend_dve, 1)
            assert m[0] == DA + 8, m[0]

            first_indices(1)
            next_indices(1, 0, 0)
            next_indices(1, 0, 1)
            combine(1, 0, 0)
            with dve.Fori(1, NG // 2) as i:
                next_indices(1, i, 0)
                combine(1, i - 1, 1)
                next_indices(1, i, 1)
                combine(1, i, 0)
            combine(1, NG // 2 - 1, 1)
            finish_stats(1, NG // 2 - 1, 1)


_INS = ['x', 'src', 'dst', 'L0_gnn_U', 'L0_gnn_Dmat', 'L0_gnn_head_w', 'L1_gnn_W_l', 'L1_gnn_b_l', 'L1_gnn_W_r']


def kernel(**inputs):
    import numpy as _np
    import concourse.bacc as _bacc
    from concourse import mybir as _mybir
    from concourse.bass_utils import run_bass_kernel_spmd as _run

    nc = _bacc.Bacc("TRN2", target_bir_lowering=False, num_devices=1,
                      dynamic_dma_scratch_size=8192)
    arrays, args = {}, []
    for name in _INS:
        a = _np.ascontiguousarray(inputs[name])
        arrays[f"in_{name}_dram"] = a
        args.append(nc.dram_tensor(f"in_{name}_dram", a.shape, _mybir.dt.from_np(a.dtype), kind="ExternalInput").ap())
    args.append(nc.dram_tensor("out_dram", inputs["x"].shape, _mybir.dt.float32, kind="ExternalOutput").ap())
    gnn_kernel(nc, *args)
    r = _run(nc, [arrays], core_ids=[0])
    return r.results[0]["out_dram"]
```

```python
from contextlib import ExitStack

import concourse.bass as bass
from concourse import mybir

P = 128
ALU = mybir.AluOpType
ACT = mybir.ActivationFunctionType
AX_X = mybir.AxisListType.X
F32 = mybir.dt.float32
I32 = mybir.dt.int32
U32 = mybir.dt.uint32

ETA, LAM = 0.5, 0.1
STEP = ETA * LAM
MIX = 0.5
LOWEST = -1.0e38
OUT_OF_RANGE = float(1 << 20)


def wait(engine, semaphore, count):
    if not isinstance(count, int) or count > 0:
        engine.wait_ge(semaphore, count)


def rounds(engine, n, body):
    body(0)
    with engine.Fori(1, n) as i:
        body(i)


def gnn_kernel(nc, x, src, dst, U, Dmat, head_w, W_l, b_l, W_r, out):
    N, D = x.shape
    E, = src.shape
    H, _, R = U.shape
    F = H * R
    KD = D // P
    NB = -(-N // P)
    GB = 7
    NG = NB // GB
    GN = GB * P
    NQ = -(-GB // 2)
    PAIRS = [range(2 * q, min(2 * q + 2, GB)) for q in range(NQ)]
    NP = NB * P
    TAIL = N - (NB - 1) * P
    C = 34
    NCH = 46
    COLS = C * NCH
    EP = COLS * P
    ELAST = E - COLS * (P - 1)
    ROW = F + 2 * H
    FW = 64
    NF = E // FW
    NK = -(-NF // FW)
    FTAIL = NF - (NK - 1) * FW
    S1 = 3
    CA = 22
    LOOK = S1 * C
    assert NG * GB == NB and NG % 2 == 0 and NCH % 2 == 0 and NG < NCH // S1 and 0 < ELAST <= COLS and NF * FW == E
    assert E <= EP and D == 2 * P

    zu_rows = nc.dram_tensor("zu_rows", (NP, F), F32, kind="Internal").ap()
    z_at_start = nc.dram_tensor("z_at_start", (EP, F), F32, kind="Internal").ap()
    rows0 = nc.dram_tensor("rows0", (EP, ROW), F32, kind="Internal").ap()
    x1 = nc.dram_tensor("x1", (NP, D), F32, kind="Internal").ap()
    rows1 = nc.dram_tensor("rows1", (EP, D), F32, kind="Internal").ap()
    own = [nc.dram_tensor(f"own{k}", (NP, D), F32, kind="Internal").ap() for k in range(2)]

    with ExitStack() as ctx:
        def sb(name, shape, dt=F32):
            return ctx.enter_context(nc.sbuf_tensor("sb_" + name, shape, dt))

        def bank(name):
            return ctx.enter_context(nc.psum_tensor("ps_" + name, [P, 512], F32))

        def sem(name):
            return ctx.enter_context(nc.semaphore(name))

        def sems(name, n):
            return [sem(f"{name}{i}") for i in range(n)]

        big = sb("big", [P, S1 * C * D])
        slot1 = [big[:, s * C * D:(s + 1) * C * D].rearrange("p (c f) -> p c f", f=D) for s in range(S1)]
        at = [0]

        def in_big(words):
            at[0] += words
            assert at[0] <= S1 * C * D
            return big[:, at[0] - words:at[0]]

        regA = in_big(4 * C * F)
        dst_i = regA[:, 2 * C * F:2 * C * F + COLS + 2].bitcast(I32)
        zero = sb("zero", [P, C * F // 4])
        zs = [regA[:, s * C * F:(s + 1) * C * F].rearrange("p (c f) -> p c f", f=F) for s in range(2)]
        zd = [regA[:, (2 + s) * C * F:(3 + s) * C * F].rearrange("p (c f) -> p c f", f=F) for s in range(2)]
        zu = in_big(NB * F).rearrange("p (b f) -> p b f", f=F)
        onehot = [in_big(GN)[0:NK, :] for _ in range(2)]
        rows0_words = in_big(2 * C * ROW)
        row0 = [rows0_words[:, s * C * ROW:(s + 1) * C * ROW].rearrange("p (c f) -> p c f", f=ROW) for s in range(2)]
        col_i = rows0_words[:, 0:COLS].bitcast(I32)
        same, ends = (rows0_words[:, k * COLS:(k + 1) * COLS] for k in (1, 2))
        Wraw = in_big(2 * KD * D).rearrange("p (w k n) -> p w k n", w=2, k=KD)
        Dm = in_big(KD * D).rearrange("p (k n) -> p k n", k=KD)
        DtD = in_big(KD * D).rearrange("p (k n) -> p k n", k=KD)
        yg = [big[:, s * GB * D:(s + 1) * GB * D].rearrange("p (b f) -> p b f", f=D) for s in range(2)]
        aggn = [big[:, 2 * GB * D + s * GB * F:2 * GB * D + (s + 1) * GB * F].rearrange("p (b f) -> p b f", f=F)
                for s in range(2)]
        turned = [big[:, 2 * GB * (D + F) + q * 2 * D:2 * GB * (D + F) + (q + 1) * 2 * D].rearrange(
            "p (j f) -> p j f", f=D) for q in range(NQ)]
        at_normed = 2 * GB * (D + F) + NQ * 2 * D
        normed = [big[:, at_normed + s * GB * D:at_normed + (s + 1) * GB * D].rearrange("p (b f) -> p b f", f=D)
                  for s in range(2)]

        xg = [sb(f"xg{s}", [P, GB, D])[:, :, :] for s in range(2)]
        hn = sb("hn", [P, 4 * GB * D])
        hg, ng1 = ([hn[:, (2 * k + s) * GB * D:(2 * k + s + 1) * GB * D].rearrange("p (b f) -> p b f", f=D)
                    for s in range(2)] for k in range(2))
        found = hn[:, 0:NB * FW].bitcast(I32).rearrange("p (b j) -> p b j", j=FW)
        ng0 = [n.rearrange("p b f -> p (b f)")[:, 0:GB * ROW].rearrange("p (b f) -> p b f", f=ROW) for n in ng1]
        tileT = [sb(f"tileT{s}", [P, 4 * P]) for s in range(2)]

        src_i = sb("src_i", [P, COLS + LOOK], I32)
        keep = sb("keep", [P, COLS])
        scratch = sb("scratch", [P, 1536])
        ident = sb("ident", [P, P])
        shift = sb("shift", [P, P])
        wrap = sb("wrap", [P, P])
        ones_row = sb("ones_row", [1, P])
        neg_step = sb("neg_step", [P, 1])
        eps = sb("eps", [P, 1])
        node_i = sb("node_i", [P, NB], I32)
        node = sb("node", [P, NB])
        part_i = sb("part_i", [P, 1], I32)
        part = sb("part", [P, 1])
        Uc = sb("Uc", [P, KD, F])
        M = sb("M", [P, KD, D])
        G = sb("G", [F, D])
        WT = sb("WT", [P, 2, KD, D])
        bias = sb("bias", [1, D])
        hw = sb("hw", [F, 3, H])
        hws = sb("hws", [F, 4])
        fence_i = sb("fence_i", [NK, FW + 2], I32)
        fence = sb("fence", [NK, FW + 1])
        lo = sb("lo", [NK, NG])
        hi = sb("hi", [NK, NG])
        fcount = sb("fcount", [P, NB])
        fbase = sb("fbase", [P, NB])
        frow = sb("frow", [P, NB])
        frow_i = sb("frow_i", [P, NB], I32)
        first = sb("first", [P, NB + 1])
        degree = sb("degree", [P, NB])
        filled = sb("filled", [P, NB])
        inv = sb("inv", [P, NB])
        tmpn = sb("tmpn", [P, NB])
        last_i = sb("last_i", [P, NB + 2 * GB], I32)
        scat_i = sb("scat_i", [P, NB], I32)
        endf = sb("endf", [P, 4])
        end_i = sb("end_i", [P, 1], I32)
        keep_all = sb("keep_all", [P, 1])
        idx = [sb(f"idx{s}", [P, C], I32) for s in range(S1)]
        nidx = [sb(f"nidx{s}", [P, GB], I32) for s in range(2)]
        zcar = sb("zcar", [P, F])
        scar = sb("scar", [P, F + H])
        logit = sb("logit", [P, H, C])
        kneg = sb("kneg", [P, C])
        keepc = sb("keepc", [P, C])
        mx = [sb(f"mx{s}", [P, H, C + 1]) for s in range(2)]
        ex = sb("ex", [P, 2, H, C])
        rec = sb("rec", [P, GB, H])
        stats = [sb(f"stats{s}", [P, GB, 6]) for s in range(2)]
        mv = [sb(f"mv{s}", [P, GB, 2]) for s in range(2)]
        rstd = [sb(f"rstd{s}", [P, GB]) for s in range(2)]
        shiftm = [sb(f"shiftm{s}", [P, GB]) for s in range(2)]
        zhead = sb("zhead", [P, F])

        got = scratch[:, 0:D]

        T = [bank("T0"), bank("T1")]
        O = [bank("O0"), bank("O1")]
        B = [bank("B0"), bank("B1")]
        Q = [bank("Q0"), bank("Q1")]
        T_of = [t[:, :].rearrange("p (j f) -> p j f", f=D) for t in T + Q]
        O_of = [t[:, :].rearrange("p (j f) -> p j f", f=D) for t in O + B]

        pads_set = sem("pads_set"); zero_set = sem("zero_set")
        fences_loaded = sem("fences_loaded"); edges_loaded = sem("edges_loaded")
        weights_loaded = sem("weights_loaded"); iotas_done = sem("iotas_done"); consts_done = sem("consts_done")
        zero_filled = sems("zero_filled", 2)
        ZERO_EARLY = NG + 3
        pads_fence = sem("pads_fence")
        xg_loaded = sems("xg_loaded", 2); xg_used = sems("xg_used", 2)
        xt_made = sem("xt_made"); xt_copied = sem("xt_copied"); zu_made = sem("zu_made"); zu_copied = sem("zu_copied")
        zu_stored = sem("zu_stored"); dve_step = sem("dve_step")
        hot_made = sems("hot_made", 2); hot_used = sems("hot_used", 2); picked_used = sems("picked_used", 2)
        hot_begun = sem("hot_begun"); compared = sem("compared"); counted = sem("counted")
        row_step = sem("row_step"); rows_known = sem("rows_known"); found_rows = sem("found_rows")
        first_known = sem("first_known"); next_made = sem("next_made"); nodes_known = sem("nodes_known")
        z_scattered = sem("z_scattered")
        zcar_loaded = sem("zcar_loaded")
        w_pe = sem("w_pe"); w_dve = sem("w_dve"); w_exp = sem("w_exp")
        idx_ready = sems("idx_ready", 2); zs_gathered = sems("zs_gathered", 2)
        zd_loaded = sems("zd_loaded", 2); zd_used = sems("zd_used", 2)
        zd_filled = sem("zd_filled"); zcar_saved = sem("zcar_saved"); product_done = sem("product_done")
        kneg_done = sem("kneg_done"); mcar_done = sem("mcar_done"); max_done = sem("max_done")
        diff_done = sem("diff_done"); exp_done = sem("exp_done"); max_stored = sem("max_stored")
        restart_added = sem("restart_added"); weighted = sem("weighted")
        sums_done = sems("sums_done", 2); scar_saved = sem("scar_saved"); rows0_stored = sems("rows0_stored", 2)
        mend_pe = sem("mend_pe"); mend_dve = sem("mend_dve"); mend_act = sem("mend_act"); mend_dma = sem("mend_dma")
        zd_begun = sem("zd_begun"); head_made = sem("head_made"); sums_begun = sem("sums_begun")
        bg_loaded = sems("bg_loaded", 2); bg_turned = sems("bg_turned", 2); bg_copied = sems("bg_copied", 2)
        bg_made = sems("bg_made", 2); bg_out = sems("bg_out", 2); bg_done = sems("bg_done", 2)
        bg_stored = sems("bg_stored", 2)

        def slot_sems(name):
            return [sems(f"{name}{layer}_", 2) for layer in range(2)]

        n_gathered = slot_sems("n_gathered"); n_loaded = slot_sems("n_loaded"); n_stored = slot_sems("n_stored")
        agg_step = sem("agg_step"); n_idx = sems("n_idx", 2); n_scaled = sem("n_scaled")
        n_turned = sems("n_turned", 2)
        n_copied = sems("n_copied", 2); n_made = sems("n_made", 2); n_taken = sems("n_taken", 2)
        n_summed = sems("n_summed", 2); n_stats = sems("n_stats", 2); n_mv = sems("n_mv", 2)
        n_std = sems("n_std", 2); n_inv = sems("n_inv", 2); n_rstd = sems("n_rstd", 2); n_normed = sems("n_normed", 2)
        idx1_ready = sems("idx1_ready", S1); r_gathered = [sems(f"r_gathered{k}_", S1) for k in range(2)]
        keepc_made = sem("keepc_made"); col_summed = sem("col_summed")
        r_stored = sems("r_stored", S1); car1_saved = sem("car1_saved")
        DA = 15
        NW = 9

        gate = sem("gate")

        block = ctx.enter_context(nc.Block())

        def edge_cols(dram, c):
            return dram.rearrange("(p c) f -> p c f", p=P)[:, bass.ds(c * C, C), :]

        def blocks(dram, g, first_block, n):
            return dram[bass.ds((g * GB + first_block) * P, n * P), :].rearrange("(b p) f -> p b f", p=P)

        def node_group(dram, g):
            return blocks(dram, g, 0, GB)

        @block.sync
        def _(sp):
            sp.wait_ge(pads_fence, 2)
            every = dst[0:E:FW]
            with nc.allow_non_contiguous_dma(reason="one word of every 64"):
                sp.dma_start(fence_i[0:NK - 1, 0:FW], every[0:(NK - 1) * FW].rearrange("(k j) -> k j", j=FW)
                             ).then_inc(fences_loaded, 16)
                sp.dma_start(fence_i[NK - 1:NK, 0:FTAIL], every[(NK - 1) * FW:NF].rearrange("(k j) -> k j", k=1)
                             ).then_inc(fences_loaded, 16)
                sp.dma_start(fence_i[0:NK - 1, FW + 1:FW + 2],
                             dst[FW * FW:FW * FW * (NK - 1) + 1:FW * FW].rearrange("(k j) -> k j", j=1)
                             ).then_inc(fences_loaded, 16)
                sp.wait_ge(pads_set, 3)
                whole = dst[0:COLS * (P - 1)].rearrange("(p c) -> p c", c=COLS)
                sp.dma_start(dst_i[0:P - 1, 1:COLS + 1], whole).then_inc(edges_loaded, 16)
                sp.dma_start(dst_i[P - 1:P, 1:ELAST + 1],
                             dst[COLS * (P - 1):E].rearrange("(p c) -> p c", p=1)).then_inc(edges_loaded, 16)
                sp.dma_start(dst_i[1:P, 0:1], whole[:, COLS - 1:COLS]).then_inc(edges_loaded, 16)
                sp.dma_start(dst_i[0:P - 1, COLS + 1:COLS + 2],
                             dst[COLS:COLS * (P - 1) + 1:COLS].rearrange("(p c) -> p c", c=1)
                             ).then_inc(edges_loaded, 16)
            sp.dma_start(src_i[0:P - 1, 0:COLS], src[0:COLS * (P - 1)].rearrange("(p c) -> p c", c=COLS)
                         ).then_inc(edges_loaded, 16)
            sp.dma_start(src_i[P - 1:P, 0:ELAST],
                         src[COLS * (P - 1):E].rearrange("(p c) -> p c", p=1)).then_inc(edges_loaded, 16)
            for h in range(H):
                sp.dma_start(Uc[:, :, h * R:(h + 1) * R], U[h].rearrange("(k p) r -> p k r", p=P)
                             ).then_inc(weights_loaded, 16)
            sp.dma_start(Dm[:, :, :], Dmat.rearrange("(k p) n -> p k n", p=P)).then_inc(weights_loaded, 16)
            sp.dma_start(Wraw[:, 0, :, :], W_l.rearrange("(k p) n -> p k n", p=P)).then_inc(weights_loaded, 16)
            sp.dma_start(Wraw[:, 1, :, :], W_r.rearrange("(k p) n -> p k n", p=P)).then_inc(weights_loaded, 16)
            sp.dma_start(bias[:, :], b_l.rearrange("(a n) -> a n", a=1)).then_inc(weights_loaded, 16)
            sp.dma_start(hw[:, 0, :], head_w.rearrange("(a n) -> a n", a=1).broadcast_to([F, H])
                         ).then_inc(weights_loaded, 16)

            def load_group(to, dram, g, done, rows=P):
                sp.dma_start(to[:, 0:GB - 1, :], blocks(dram, g, 0, GB - 1)).then_inc(done, 16)
                sp.dma_start(to[0:rows, GB - 1, :], dram[bass.ds((g * GB + GB - 1) * P, rows), :]
                             ).then_inc(done, 16)

            def load_x(i, s, rows=P):
                wait(sp, xg_used[s], i)
                load_group(xg[s], x, 2 * i + s, xg_loaded[s], rows)

            def store_zu(i, s):
                sp.wait_ge(zu_copied, 2 * i + s + 1)
                sp.dma_start(node_group(zu_rows, 2 * i + s), zu[:, bass.ds((2 * i + s) * GB, GB), :]
                             ).then_inc(zu_stored, 16)

            load_x(0, 0)
            load_x(0, 1)
            with sp.Fori(1, NG // 2 - 1) as i:
                for s in range(2):
                    load_x(i, s)
                for s in range(2):
                    store_zu(i - 1, s)
            load_x(NG // 2 - 1, 0)
            load_x(NG // 2 - 1, 1, rows=TAIL)
            for i in (NG // 2 - 2, NG // 2 - 1):
                for s in range(2):
                    store_zu(i, s)

            def bg_load(layer, g, rows=P):
                wait(sp, bg_done[layer], g)
                load_group(xg[0], x if layer == 0 else x1, g, bg_loaded[layer], rows)

            def bg_store(layer, g):
                sp.wait_ge(bg_done[layer], g + 1)
                sp.dma_start(node_group(own[layer], g), hg[0]).then_inc(bg_stored[layer], 16)

            sp.wait_ge(z_scattered, 16 * NB)
            sp.wait_ge(zcar_loaded, 16)

            def load_zd(i):
                for s in range(2):
                    wait(sp, zd_used[s], i)
                    sp.dma_start(zd[s], edge_cols(z_at_start, 2 * i + s)).then_inc(zd_loaded[s], 16)

            load_zd(0)
            bg_load(0, 0)
            with sp.Fori(1, NG - 1) as i:
                load_zd(i)
                bg_store(0, i - 1)
                bg_load(0, i)
            load_zd(NG - 1)
            bg_store(0, NG - 2)
            bg_load(0, NG - 1, rows=TAIL)
            load_zd(NG)
            bg_store(0, NG - 1)
            with sp.Fori(NG + 1, NCH // 2) as i:
                load_zd(i)

            def node_in(layer, i, s, rows=P):
                g = 2 * i + s
                wait(sp, n_made[0] if layer == 0 else n_summed[1], NQ * (g - 1))
                sp.dma_start(yg[s], node_group(own[layer], g)).then_inc(n_loaded[layer][s], 16)
                if layer == 0:
                    wait(sp, n_summed[0], NQ * (g - 1))
                load_group(xg[s], x if layer == 0 else x1, g, n_loaded[layer][s], rows)

            def node_phase(layer):
                sp.wait_ge(bg_stored[layer], 16 * NG)
                for s in range(2):
                    node_in(layer, 0, s)
                with sp.Fori(1, NG // 2 - 1) as i:
                    for s in range(2):
                        node_in(layer, i, s)
                node_in(layer, NG // 2 - 1, 0)
                node_in(layer, NG // 2 - 1, 1, rows=TAIL if layer == 0 else P)

            sp.wait_ge(mend_dma, 32)
            node_phase(0)
            for s in range(2):
                sp.wait_ge(n_stored[0][s], 32 * (NG // 2))

            def store_rows1(i, s):
                c = S1 * i + s
                sp.wait_ge(col_summed, c * C + CA)
                sp.dma_start(edge_cols(rows1, c)[:, 0:CA, :], slot1[s][:, 0:CA, :]).then_inc(r_stored[s], 16)
                sp.wait_ge(car1_saved, c + 2)
                sp.dma_start(edge_cols(rows1, c)[:, CA:C, :], slot1[s][:, CA:C, :]).then_inc(r_stored[s], 16)

            bg_load(1, 0)
            for s in range(S1):
                store_rows1(0, s)
            with sp.Fori(1, NG) as i:
                bg_store(1, i - 1)
                bg_load(1, i)
                for s in range(S1):
                    store_rows1(i, s)
            bg_store(1, NG - 1)
            for k in range(S1 * NG, NCH):
                store_rows1(k // S1, k % S1)
            sp.wait_ge(mend_dma, 64)
            node_phase(1)
            for s in range(2):
                sp.wait_ge(n_stored[1][s], 32 * (NG // 2))

        @block.gpsimd
        def _(pool):
            pool.iota(node_i[:, :], pattern=[[P, NB]], base=0, channel_multiplier=1).then_inc(iotas_done, 1)
            pool.iota(part_i[:, :], pattern=[[0, 1]], base=0, channel_multiplier=COLS).then_inc(iotas_done, 1)
            pool.iota(scratch[:, 512:512 + GN].bitcast(I32), pattern=[[1, GN]], base=0, channel_multiplier=0
                      ).then_inc(iotas_done, 1)
            pool.iota(col_i, pattern=[[1, COLS]], base=0, channel_multiplier=0
                      ).then_inc(iotas_done, 1)
            pool.iota(fence_i[:, FW:FW + 1], pattern=[[0, 1]], base=0, channel_multiplier=FW
                      ).then_inc(iotas_done, 1)
            for m in (ident, shift, wrap):
                pool.memset(m[:, :], 0.0).then_inc(consts_done, 1)
            pool.wait_ge(consts_done, 3)
            for m, base, step in ((ident, 0, -1), (shift, -1, -1)):
                pool.affine_select(out=m[:, :], in_=m[:, :], compare_op=ALU.not_equal, fill=1.0, base=base,
                                   pattern=[[step, P]], channel_multiplier=1).then_inc(consts_done, 1)
            pool.affine_select(out=wrap[:, :], in_=wrap[:, :], compare_op=ALU.not_equal, fill=1.0, base=P - 1,
                               pattern=[[-1, P]], channel_multiplier=P).then_inc(consts_done, 1)

            def gather(to, table, index, done, limit=None):
                more = {} if limit is None else dict(bounds_check=limit, oob_is_err=False)
                pool.indirect_dma_start(to, None, table, bass.IndirectOffsetOnAxis(ap=index.bitcast(U32), axis=0),
                                        **more).then_inc(done, 16)

            dst_rows = dst.rearrange("(r j) -> r j", j=FW)
            for g in range(NG):
                pool.wait_ge(rows_known, g + 1)
                for b in range(g * GB, (g + 1) * GB):
                    gather(found[:, b, :], dst_rows, frow_i[:, b:b + 1], found_rows)

            def gather_zs(i, s):
                pool.wait_ge(idx_ready[s], i + 1)
                wait(pool, sums_done[s], i)
                pool.sem_inc(gate, 1)
                for j in range(C):
                    gather(zs[s][:, j, :], zu_rows, idx[s][:, j:j + 1], zs_gathered[s])

            pool.wait_ge(zu_stored, 16 * NG)
            gather_zs(0, 0)
            pool.wait_ge(nodes_known, 1)
            for q in range(2):
                pool.wait_ge(zero_filled[q], 16 * (NCH // 2))
            for b in range(NB):
                first_edges = bass.IndirectOffsetOnAxis(ap=scat_i[:, b:b + 1].bitcast(U32), axis=0)
                pool.indirect_dma_start(z_at_start, first_edges,
                                        zu[:, b, :], None, bounds_check=EP - 1, oob_is_err=False
                                        ).then_inc(z_scattered, 16)
            gather(zcar[:, :], zu_rows, dst_i[:, 1:2], zcar_loaded)
            gather_zs(0, 1)
            with pool.Fori(1, NCH // 2) as i:
                for s in range(2):
                    gather_zs(i, s)

            for s in range(2):
                pool.wait_ge(rows0_stored[s], 16 * (NCH // 2))
            pool.wait_ge(mend_dve, 1)
            gather(got[:, 0:ROW], rows0, end_i[:, 0:1], mend_dma, EP - 1)
            pool.wait_ge(mend_dve, DA)
            pool.indirect_dma_start(rows0, bass.IndirectOffsetOnAxis(ap=end_i[:, 0:1].bitcast(U32), axis=0),
                                    got[:, 0:ROW], None, bounds_check=EP - 1, oob_is_err=False
                                    ).then_inc(mend_dma, 16)
            pool.wait_ge(mend_dma, 32)

            def node_gathers(layer):
                def body(i):
                    for s in range(2):
                        g = 2 * i + s
                        pool.wait_ge(n_idx[layer], g + 1)
                        wait(pool, n_scaled if layer == 0 else n_turned[1], g - 1 if layer == 0 else NQ * (g - 1))
                        pool.sem_inc(gate, 1)
                        for b in range(GB):
                            to, table = (ng0, rows0) if layer == 0 else (ng1, rows1)
                            gather(to[s][:, b, :], table, nidx[s][:, b:b + 1], n_gathered[layer][s])
                rounds(pool, NG // 2, body)

            node_gathers(0)

            for s in range(2):
                pool.wait_ge(n_stored[0][s], 32 * (NG // 2))

            def gather_rows1(i, s):
                pool.wait_ge(idx1_ready[s], i + 1)
                wait(pool, r_stored[s], 32 * i)
                pool.sem_inc(gate, 1)
                for j in range(C):
                    gather(slot1[s][:, j, :], x1, idx[s][:, j:j + 1], r_gathered[int(j >= CA)][s])

            rounds(pool, NCH // S1, lambda i: [gather_rows1(i, s) for s in range(S1)])
            for s in range(NCH % S1):
                gather_rows1(NCH // S1, s)

            for s in range(S1):
                pool.wait_ge(r_stored[s], 32 * (NCH // S1 + (s < NCH % S1)))
            pool.wait_ge(mend_dve, DA + 1)
            gather(got[:, :], rows1, end_i[:, 0:1], mend_dma, EP - 1)
            pool.wait_ge(mend_dve, DA + 9)
            pool.indirect_dma_start(rows1, bass.IndirectOffsetOnAxis(ap=end_i[:, 0:1].bitcast(U32), axis=0),
                                    got[:, :], None, bounds_check=EP - 1, oob_is_err=False
                                    ).then_inc(mend_dma, 16)
            pool.wait_ge(mend_dma, 64)
            node_gathers(1)

        @block.tensor
        def _(pe):
            pe.wait_ge(consts_done, 6)

            def pick(i):
                for s in range(2):
                    pe.wait_ge(hot_made[s], i + 1)
                    wait(pe, picked_used[s], i)
                    for b in range(GB):
                        mm = pe.matmul(Q[s][:, b * (FW + 1):(b + 1) * (FW + 1)], onehot[s][:, b * P:(b + 1) * P],
                                       fence[:, :], start=True, stop=True)
                    mm.then_inc(hot_used[s], 1)

            def project(i):
                if isinstance(i, int):
                    pe.wait_ge(weights_loaded, 16 * NW)
                for n in range(2 * NQ + 1):
                    if n < 2 * NQ:
                        s, q = n // NQ, n % NQ
                        if q == 0:
                            pe.wait_ge(xg_loaded[s], 32 * (i + 1))
                        for j, b in enumerate(PAIRS[q]):
                            for k in range(KD):
                                mm = pe.transpose(T[n % 2][:, j * D + k * P:j * D + (k + 1) * P],
                                                  xg[s][:, b, k * P:(k + 1) * P], ident[:, :])
                        mm.then_inc(xt_made, 1)
                    if n > 0:
                        m, s, q = n - 1, (n - 1) // NQ, (n - 1) % NQ
                        if m == 0:
                            wait(pe, zu_copied, 2 * i)
                        pe.wait_ge(xt_copied, 2 * NQ * i + m + 1)
                        for j, b in enumerate(PAIRS[q]):
                            for k in range(KD):
                                mm = pe.matmul(B[s][:, b * F:(b + 1) * F],
                                               tileT[m % 2][:, j * D + k * P:j * D + (k + 1) * P], Uc[:, k, :],
                                               start=(k == 0), stop=(k == KD - 1))
                        if q == NQ - 1:
                            mm.then_inc(zu_made, 1)

            rounds(pe, NG // 2, lambda i: (pick(i), project(i)))

            for m in range(KD):
                for k in range(KD):
                    mm = pe.matmul(O[0][:, m * D:(m + 1) * D], Dm[:, k, m * P:(m + 1) * P], Dm[:, k, :],
                                   start=(k == 0), stop=(k == KD - 1))
            mm.then_inc(w_pe, 1)
            pe.wait_ge(w_dve, 1)
            for m in range(KD):
                for k in range(KD):
                    mm = pe.matmul(O[1][:, m * D:(m + 1) * D], DtD[:, k, m * P:(m + 1) * P], Dm[:, k, :],
                                   start=(k == 0), stop=(k == KD - 1))
            mm.then_inc(w_pe, 1)
            for w in range(2):
                if w == 1:
                    pe.wait_ge(w_dve, 2)
                for k in range(KD):
                    for m in range(KD):
                        mm = pe.transpose(O[0][:, k * D + m * P:k * D + (m + 1) * P],
                                          Wraw[:, w, m, k * P:(k + 1) * P], ident[:, :])
                mm.then_inc(w_pe, 1)
            pe.wait_ge(w_dve, 6)
            for k in range(KD):
                mm = pe.matmul(O[1][0:F, 0:D], Uc[:, k, :], M[:, k, :], start=(k == 0), stop=(k == KD - 1))
            mm.then_inc(w_pe, 1)

            pe.wait_ge(first_known, 1)
            pe.matmul(Q[0][:, 0:NB], shift[:, :], first[:, 0:NB], start=True, stop=False)
            pe.matmul(Q[0][:, 0:NB], wrap[:, :], first[:, 1:NB + 1], start=False, stop=True).then_inc(next_made, 1)

            def background(layer):
                right_of = M if layer == 0 else WT[:, 1]

                def body(g):
                    pe.wait_ge(bg_loaded[layer], 32 * (g + 1))
                    for b in range(GB + 1):
                        if b < GB:
                            wait(pe, bg_copied[layer], GB * g + max(b - 1, 0))
                            for k in range(KD):
                                mm = pe.transpose(T[b % 2][:, k * P:(k + 1) * P], xg[0][:, b, k * P:(k + 1) * P],
                                                  ident[:, :])
                            mm.then_inc(bg_turned[layer], 1)
                        if b > 0:
                            m = b - 1
                            o = O[m % 2][:, 0:D]
                            wait(pe, bg_out[layer], GB * g + max(m - 1, 0))
                            if layer == 1:
                                pe.matmul(o, ones_row[:, :], bias[:, :], start=True, stop=False)
                            pe.wait_ge(bg_copied[layer], GB * g + m + 1)
                            for k in range(KD):
                                mm = pe.matmul(o, tileT[m % 2][:, k * P:(k + 1) * P], right_of[:, k, :],
                                               start=(layer == 0 and k == 0), stop=(k == KD - 1))
                            mm.then_inc(bg_made[layer], 1)

                rounds(pe, NG, body)

            pe.wait_ge(w_dve, 9 + 2 * KD)
            background(0)

            pe.wait_ge(mend_dve, 5)
            for k in range(4):
                mm = pe.transpose(T[0][0:F, k * P:(k + 1) * P], scratch[:, 512 + k * F:512 + (k + 1) * F],
                                  ident[:, :])
            mm.then_inc(mend_pe, 1)
            pe.wait_ge(mend_dve, 10)
            for k in range(3):
                mm = pe.transpose(T[1][:, k * F:(k + 1) * F], scratch[0:F, 1024 + k * (P + 1):1024 + k * (P + 1) + P],
                                  ident[0:F, 0:F])
            mm.then_inc(mend_pe, 1)

            def dense(layer):
                parts = 1 if layer == 0 else KD
                width = F if layer == 0 else P

                def body(i):
                    for s in range(2):
                        g = 2 * i + s
                        pe.wait_ge(n_scaled if layer == 0 else n_gathered[1][s],
                                   g + 1 if layer == 0 else 16 * GB * (i + 1))
                        for q in range(NQ):
                            wait(pe, n_copied[layer], NQ * (g - 1) + q + 1)
                            pe.sem_inc(gate, 1)
                            of = aggn[s] if layer == 0 else ng1[s]
                            for j, b in enumerate(PAIRS[q]):
                                for k in range(parts):
                                    mm = pe.transpose(T_of[q][0:width, j, k * P:(k + 1) * P],
                                                      of[:, b, k * width:(k + 1) * width], ident[:, :])
                            mm.then_inc(n_turned[layer], 1)
                        for q in range(NQ):
                            wait(pe, n_taken[layer], NQ * (g - 1) + q + 1)
                            if layer == 0 and q == 0:
                                pe.wait_ge(n_loaded[layer][s], 48 * (i + 1))
                            pe.wait_ge(n_copied[layer], NQ * g + q + 1)
                            for j, b in enumerate(PAIRS[q]):
                                if layer == 0:
                                    pe.matmul(O_of[q][:, j, :], ident[:, :], yg[s][:, b, :], start=True, stop=False)
                                for k in range(parts):
                                    mm = pe.matmul(O_of[q][:, j, :], turned[q][0:width, j, k * P:(k + 1) * P],
                                                   G[:, :] if layer == 0 else WT[:, 0, k, :],
                                                   start=(layer == 1 and k == 0), stop=(k == parts - 1))
                            mm.then_inc(n_made[layer], 1)

                rounds(pe, NG // 2, body)

            dense(0)
            background(1)

            pe.wait_ge(mend_dve, DA + 3)
            for k in range(KD):
                mm = pe.transpose(T[0][:, k * P:(k + 1) * P], scratch[:, 512 + k * P:512 + (k + 1) * P], ident[:, :])
            mm = pe.transpose(T[0][:, KD * P:(KD + 1) * P], scratch[:, 512 + KD * P:512 + (KD + 1) * P], ident[:, :])
            mm.then_inc(mend_pe, 1)
            pe.wait_ge(mend_dve, DA + 7)
            for k in range(KD):
                mm = pe.transpose(T[1][:, k * P:(k + 1) * P], scratch[:, 1024 + k * (P + 1):1024 + k * (P + 1) + P],
                                  ident[:, :])
            mm.then_inc(mend_pe, 1)

            dense(1)

        @block.scalar
        def _(act):
            z_flat = z_at_start.rearrange("(p a) f -> p (a f)", p=P)

            def fill(k, q):
                wait(act, zero_filled[q], 16 * k)
                k = 2 * k + q
                act.dma_start(z_flat[:, bass.ds(k * C * F, C * F)].rearrange("p (a c) -> p a c", a=4),
                              zero[:, :].unsqueeze(1).broadcast_to([P, 4, C * F // 4])).then_inc(zero_filled[q], 16)

            act.wait_ge(zero_set, 1)
            def project(i):
                for s in range(2):
                    for q in range(NQ):
                        if q % 2 == 0:
                            fill(2 * i + s, q // 2)
                        n, width = s * NQ + q, len(PAIRS[q]) * D
                        act.wait_ge(xt_made, 2 * NQ * i + n + 1)
                        act.copy(tileT[n % 2][:, 0:width], T[n % 2][:, 0:width]).then_inc(xt_copied, 1)
                    act.sem_inc(xg_used[s], 1)
                    act.wait_ge(zu_made, 2 * i + s + 1)
                    act.copy(zu[:, bass.ds((2 * i + s) * GB, GB), :],
                             B[s][:, 0:GB * F].rearrange("p (b f) -> p b f", f=F)).then_inc(zu_copied, 1)

            rounds(act, NG // 2, project)
            act.wait_ge(edges_loaded, 16 * 6)
            for s in range(2):
                act.copy(idx[s][:, :], src_i[:, s * C:(s + 1) * C]).then_inc(idx_ready[s], 1)
            with act.Fori(NG, ZERO_EARLY) as k:
                for q in range(2):
                    fill(k, q)

            act.wait_ge(w_dve, 8)
            act.activation(hw[:, 1, :], hw[:, 0, :], ACT.Exp, bias=hws[:, 0:1]).then_inc(w_exp, 1)

            with act.Fori(ZERO_EARLY, NCH // 2) as k:
                for q in range(2):
                    fill(k, q)

            def background(layer, g):
                for b in range(GB + 1):
                    if b < GB:
                        act.wait_ge(bg_turned[layer], GB * g + b + 1)
                        act.copy(tileT[b % 2][:, 0:KD * P], T[b % 2][:, 0:KD * P]).then_inc(bg_copied[layer], 1)
                    if b == 0:
                        wait(act, bg_stored[layer], 16 * g)
                    else:
                        act.wait_ge(bg_made[layer], GB * g + b)
                        to, o = hg[0][:, b - 1, :], O[(b - 1) % 2][:, 0:D]
                        if layer == 0:
                            ins = act.activation(to, o, ACT.Identity, bias=neg_step[:, 0:1])
                        else:
                            ins = act.copy(to, o)
                        ins.then_inc(bg_out[layer], 1)
                act.wait_ge(bg_out[layer], GB * (g + 1))
                act.sem_inc(bg_done[layer], 1)

            def weights_of_edges(i, with_background):
                for s in range(2):
                    act.wait_ge(diff_done, 2 * (2 * i + s + 1))
                    act.activation(ex[:, :, :, :].rearrange("p a h c -> p (a h c)"),
                                   ex[:, :, :, :].rearrange("p a h c -> p (a h c)"), ACT.Exp,
                                   scale=1.0 / float(R) ** 0.5).then_inc(exp_done, 1)
                    wait(act, rows0_stored[s], 16 * i)
                    act.copy(row0[s][:, :, F + H:ROW], mx[s][:, :, 1:C + 1].rearrange("p h c -> p c h")
                             ).then_inc(max_stored, 1)
                    act.wait_ge(sums_done[s], i + 1)
                    act.wait_ge(max_stored, 2 * i + s + 1)
                    act.dma_start(edge_cols(rows0, 2 * i + s), row0[s]).then_inc(rows0_stored[s], 16)
                    act.wait_ge(zs_gathered[s], 16 * C * (i + 1))
                    act.copy(idx[s][:, :], src_i[:, bass.ds((2 * i + s + 2) * C, C)]).then_inc(idx_ready[s], 1)
                    if with_background and s == 0:
                        background(0, i)

            weights_of_edges(0, True)
            with act.Fori(1, NG) as i:
                weights_of_edges(i, True)
            with act.Fori(NG, NCH // 2) as i:
                weights_of_edges(i, False)

            scale = 1.0 / float(R) ** 0.5
            act.wait_ge(mend_dve, 8)
            act.activation(scratch[0:F, 512:512 + 2 * P], scratch[0:F, 512:512 + 2 * P], ACT.Exp, scale=scale
                           ).then_inc(mend_act, 1)
            act.wait_ge(mend_dve, 13)
            act.activation(scratch[:, 512:512 + 2 * F], scratch[:, 512:512 + 2 * F], ACT.Exp, scale=scale
                           ).then_inc(mend_act, 1)

            def node_groups(layer):
                width, part = (P, F) if layer == 0 else (KD * P, P)

                def std(i, s):
                    act.wait_ge(n_mv[layer], GB * (2 * i + s + 1))
                    act.activation(rstd[s][:, :], mv[s][:, :, 1], ACT.Sqrt, bias=eps[:, 0:1]
                                   ).then_inc(n_std[layer], 1)

                def norm(i, s, b):
                    if b == 0:
                        act.wait_ge(n_rstd[layer], 2 * i + s + 1)
                        wait(act, n_stored[layer][s], 32 * i)
                    done = act.activation(normed[s][:, b, :], hg[s][:, b, :], ACT.Identity,
                                          bias=shiftm[s][:, b:b + 1], scale=rstd[s][:, b:b + 1])
                    if b == GB - 1:
                        done.then_inc(n_normed[layer], 1)

                def store(i, s, rows=P):
                    g = 2 * i + s
                    dram = x1 if layer == 0 else out
                    act.wait_ge(n_normed[layer], g + 1)
                    act.dma_start(blocks(dram, g, 0, GB - 1), normed[s][:, 0:GB - 1, :]
                                  ).then_inc(n_stored[layer][s], 16)
                    act.dma_start(dram[bass.ds((g * GB + GB - 1) * P, rows), :], normed[s][0:rows, GB - 1, :]
                                  ).then_inc(n_stored[layer][s], 16)

                def body(i):
                    for s in range(2):
                        g = 2 * i + s
                        there = not isinstance(i, int) or i > 0
                        if there:
                            std(i - 1, s)
                        for q in range(NQ):
                            act.wait_ge(n_turned[layer], NQ * g + q + 1)
                            wait(act, n_made[layer], NQ * (g - 1) + q + 1)
                            n = len(PAIRS[q])
                            act.copy(turned[q][0:part, 0:n, 0:width], T_of[q][0:part, 0:n, 0:width]
                                     ).then_inc(n_copied[layer], 1)
                            if there and q > 0:
                                for b in PAIRS[q - 1]:
                                    norm(i - 1, s, b)
                        if there:
                            norm(i - 1, s, GB - 1)
                            store(i - 1, s)

                rounds(act, NG // 2, body)
                for s in range(2):
                    std(NG // 2 - 1, s)
                    for b in range(GB):
                        norm(NG // 2 - 1, s, b)
                    store(NG // 2 - 1, s, rows=P if layer == 0 or s == 0 else TAIL)

            node_groups(0)
            rounds(act, NG, lambda g: background(1, g))
            node_groups(1)

        @block.vector
        def _(dve):
            steps = [0]

            def done(ins, which=dve_step):
                steps[0] += 1
                ins.then_inc(dve_step, 1)
                dve.wait_ge(dve_step, steps[0])

            dve.memset(fence_i[:, 0:FW], 1 << 20).then_inc(pads_fence, 1)
            dve.memset(fence_i[:, FW + 1:FW + 2], 1 << 20).then_inc(pads_fence, 1)
            dve.memset(dst_i[:, 1:COLS + 2], N).then_inc(pads_set, 1)
            dve.memset(dst_i[:, 0:1], -1).then_inc(pads_set, 1)
            dve.memset(src_i[:, :], 0).then_inc(pads_set, 1)
            dve.memset(zero[:, :], 0.0).then_inc(zero_set, 1)
            dve.memset(last_i[:, NB:NB + 2 * GB], 0)
            dve.memset(neg_step[:, :], -ETA * LAM)
            dve.memset(eps[:, :], 1e-5)
            dve.memset(ones_row[:, :], 1.0)
            dve.memset(first[:, NB:NB + 1], float(E))
            dve.wait_ge(iotas_done, 5)
            dve.tensor_copy(node[:, :], node_i[:, :])
            dve.tensor_copy(part[:, :], part_i[:, :])
            count = scratch[:, 512:512 + GN].bitcast(I32)

            dve.wait_ge(fences_loaded, 48)
            dve.tensor_copy(fence[:, :], fence_i[:, 0:FW + 1])
            done(dve.tensor_copy(hi[:, 0:1], fence_i[:, FW + 1:FW + 2]))
            done(dve.tensor_copy(lo[:, 0:1], fence[:, 0:1]))
            done(dve.memset(lo[0:1, 0:1], -1.0))
            for g in range(1, NG):
                dve.tensor_scalar(lo[:, g:g + 1], lo[:, 0:1], float(-g * GN), None, ALU.add)
                ins = dve.tensor_scalar(hi[:, g:g + 1], hi[:, 0:1], float(-g * GN), None, ALU.add)
            done(ins)

            def make_hot(i, s):
                g = 2 * i + s
                wait(dve, hot_used[s], i)
                dve.tensor_scalar(onehot[s], count[0:NK, :], hi[:, bass.ds(g, 1)], None, ALU.is_gt
                                  ).then_inc(hot_begun, 1)
                dve.wait_ge(hot_begun, g + 1)
                dve.scalar_tensor_tensor(out=onehot[s], in0=count[0:NK, :], scalar=lo[:, bass.ds(g, 1)],
                                         in1=onehot[s], op0=ALU.is_gt, op1=ALU.subtract).then_inc(hot_made[s], 1)

            def count_fences(i, s):
                g = 2 * i + s
                dve.wait_ge(hot_used[s], i + 1)
                q = Q[s][:, 0:GB * (FW + 1)].rearrange("p (b j) -> p b j", j=FW + 1)
                less = scratch[:, 0:GB * FW].rearrange("p (b j) -> p b j", j=FW)
                who = node[:, bass.ds(g * GB, GB)].unsqueeze(2).broadcast_to([P, GB, FW])
                wait(dve, counted, g)
                dve.tensor_tensor(less, q[:, :, 0:FW], who, ALU.is_lt).then_inc(compared, 1)
                dve.tensor_copy(fbase[:, bass.ds(g * GB, GB)], q[:, :, FW]).then_inc(picked_used[s], 1)
                dve.wait_ge(compared, g + 1)
                own_blocks = bass.ds(g * GB, GB)
                dve.tensor_reduce(fcount[:, own_blocks], less, AX_X, ALU.add).then_inc(counted, 1)
                dve.wait_ge(counted, g + 1)
                dve.wait_ge(picked_used[s], i + 1)
                dve.scalar_tensor_tensor(out=frow[:, own_blocks], in0=fcount[:, own_blocks], scalar=-1.0,
                                         in1=fbase[:, own_blocks], op0=ALU.add, op1=ALU.add).then_inc(row_step, 1)
                dve.wait_ge(row_step, 2 * g + 1)
                dve.tensor_scalar(frow[:, own_blocks], frow[:, own_blocks], 0.0, None, ALU.max).then_inc(row_step, 1)
                dve.wait_ge(row_step, 2 * g + 2)
                dve.tensor_copy(frow_i[:, own_blocks], frow[:, own_blocks]).then_inc(rows_known, 1)

            make_hot(0, 0)
            make_hot(0, 1)
            count_fences(0, 0)
            with dve.Fori(1, NG // 2) as i:
                make_hot(i, 0)
                count_fences(i - 1, 1)
                make_hot(i, 1)
                count_fences(i, 0)
            count_fences(NG // 2 - 1, 1)

            dve.wait_ge(edges_loaded, 16 * 6)
            dve.tensor_tensor(keep[:, :], dst_i[:, 1:COLS + 1], dst_i[:, 0:COLS], ALU.is_equal)
            dve.tensor_copy(ends, col_i)
            done(dve.tensor_tensor(same, dst_i[:, 1:COLS + 1], dst_i[:, 2:COLS + 2], ALU.is_equal))
            done(dve.scalar_tensor_tensor(out=ends, in0=same, scalar=OUT_OF_RANGE, in1=ends, op0=ALU.mult,
                                          op1=ALU.add))
            dve.tensor_reduce(keep_all[:, :], keep[:, :], AX_X, ALU.min)
            done(dve.tensor_reduce(endf[:, 0:1], ends, AX_X, ALU.min))
            done(dve.tensor_scalar(endf[:, 1:2], keep[:, 0:1], -1.0, -OUT_OF_RANGE, ALU.add, ALU.mult))
            done(dve.scalar_tensor_tensor(out=endf[:, 2:3], in0=endf[:, 0:1], scalar=part[:, 0:1], in1=endf[:, 1:2],
                                          op0=ALU.add, op1=ALU.add))
            done(dve.tensor_copy(end_i[:, :], endf[:, 2:3]))

            dve.wait_ge(weights_loaded, 16 * NW)
            dve.wait_ge(w_pe, 1)
            dve.tensor_copy(DtD[:, :, :].rearrange("p k n -> p (k n)"), O[0][:, :]).then_inc(w_dve, 1)
            for w in range(2):
                dve.wait_ge(w_pe, 3 + w)
                dve.tensor_copy(WT[:, w, :, :].rearrange("p k n -> p (k n)"), O[0][:, :]).then_inc(w_dve, 1)
            done(dve.scalar_tensor_tensor(out=M[:, :, :].rearrange("p k n -> p (k n)"), in0=O[1][:, :], scalar=-1.0,
                                          in1=Dm[:, :, :].rearrange("p k n -> p (k n)"), op0=ALU.mult, op1=ALU.add))
            done(dve.tensor_scalar(M[:, :, :].rearrange("p k n -> p (k n)"), M[:, :, :].rearrange("p k n -> p (k n)"),
                                   MIX * ETA, None, ALU.mult))
            dve.wait_ge(consts_done, 6)
            for k in range(KD):
                dve.scalar_tensor_tensor(out=M[:, k, k * P:(k + 1) * P], in0=ident[:, :], scalar=MIX,
                                         in1=M[:, k, k * P:(k + 1) * P], op0=ALU.mult, op1=ALU.add
                                         ).then_inc(w_dve, 1)
            dve.tensor_scalar(hws[:, 1:2], part[0:F, :], 1.0 / COLS, None, ALU.mult).then_inc(w_dve, 1)
            dve.wait_ge(w_dve, 6)
            done(dve.tensor_reduce(hws[:, 2:3], hw[:, 0, :], AX_X, ALU.max))
            done(dve.tensor_scalar(hws[:, 0:1], hws[:, 2:3], -1.0, None, ALU.mult))
            for h in range(H):
                ins = dve.tensor_scalar(hw[:, 2, h:h + 1], hws[:, 1:2], float(h * R) - 0.5, None, ALU.is_gt)
            done(ins)
            dve.sem_inc(w_dve, 2)
            done(dve.tensor_tensor(hw[:, 2, 0:H - 1], hw[:, 2, 0:H - 1], hw[:, 2, 1:H], ALU.subtract))
            dve.wait_ge(w_exp, 1)
            dve.tensor_reduce(hws[:, 2:3], hw[:, 1, :], AX_X, ALU.add)
            done(dve.tensor_tensor(hw[:, 0, :], hw[:, 1, :], hw[:, 2, :], ALU.mult))
            done(dve.tensor_reduce(hws[:, 3:4], hw[:, 0, :], AX_X, ALU.add))
            done(dve.reciprocal(hws[:, 2:3], hws[:, 2:3]))
            done(dve.tensor_tensor(hws[:, 3:4], hws[:, 3:4], hws[:, 2:3], ALU.mult))
            dve.wait_ge(w_pe, 5)
            dve.tensor_scalar(G[0:F, :], O[1][0:F, 0:D], hws[:, 3:4], None, ALU.mult).then_inc(w_dve, 1)
            for to, times in ((M, 1.0), (WT[:, 1], 2.0)):
                for k in range(KD):
                    dve.scalar_tensor_tensor(out=to[:, k, k * P:(k + 1) * P], in0=ident[:, :], scalar=times,
                                             in1=to[:, k, k * P:(k + 1) * P], op0=ALU.mult, op1=ALU.add
                                             ).then_inc(w_dve, 1)

            dve.wait_ge(found_rows, 16 * NB)
            for g in range(NG):
                less = scratch[:, 0:GB * FW].rearrange("p (b j) -> p b j", j=FW)
                who = node[:, g * GB:(g + 1) * GB].unsqueeze(2).broadcast_to([P, GB, FW])
                done(dve.tensor_tensor(less, found[:, g * GB:(g + 1) * GB, :], who, ALU.is_lt))
                done(dve.tensor_reduce(fcount[:, g * GB:(g + 1) * GB], less, AX_X, ALU.add))
            dve.scalar_tensor_tensor(out=first[:, 0:NB], in0=frow[:, :], scalar=float(FW), in1=fcount[:, :],
                                     op0=ALU.mult, op1=ALU.add).then_inc(first_known, 1)
            dve.wait_ge(next_made, 1)
            done(dve.tensor_tensor(degree[:, :], Q[0][:, 0:NB], first[:, 0:NB], ALU.subtract))
            dve.tensor_scalar(filled[:, :], degree[:, :], 0.0, None, ALU.is_gt)
            dve.tensor_scalar(last_i[:, 0:NB], Q[0][:, 0:NB], -1.0, 0.0, ALU.add, ALU.max)
            done(dve.tensor_scalar(inv[:, :], degree[:, :], 1.0, None, ALU.max))
            dve.tensor_scalar(tmpn[:, :], filled[:, :], -1.0, -OUT_OF_RANGE, ALU.add, ALU.mult)
            done(dve.reciprocal(inv[:, :], inv[:, :]))
            dve.tensor_tensor(inv[:, :], inv[:, :], filled[:, :], ALU.mult)
            dve.tensor_tensor(scat_i[:, :], first[:, 0:NB], tmpn[:, :], ALU.add).then_inc(nodes_known, 1)

            dve.memset(scar[:, :], 0.0)
            done(dve.memset(mx[1][:, :, C:C + 1], LOWEST))
            dve.wait_ge(zcar_loaded, 16)

            def edge_chunks(i):
                for s in range(2):
                    c = 2 * i + s
                    kp = keep[:, bass.ds(c * C, C)]
                    kp0 = keep[:, bass.ds(c * C, 1)]
                    dve.wait_ge(zd_loaded[s], 16 * (i + 1))
                    wait(dve, zcar_saved, c)
                    dve.scalar_tensor_tensor(out=zd[s][:, 0, :], in0=zcar[:, :], scalar=kp0, in1=zd[s][:, 0, :],
                                             op0=ALU.mult, op1=ALU.add).then_inc(zd_begun, 1)
                    dve.tensor_scalar(kneg[:, :], kp, -1.0, -LOWEST, ALU.add, ALU.mult).then_inc(kneg_done, 1)
                    dve.tensor_copy(mx[s][:, :, 0:1], mx[1 - s][:, :, C:C + 1]).then_inc(mcar_done, 1)
                    dve.wait_ge(zd_begun, c + 1)
                    for f in range(F):
                        ins = dve.tensor_tensor_scan(zd[s][:, :, f], kp, zd[s][:, :, f], 0.0, ALU.mult, ALU.add)
                    ins.then_inc(zd_filled, 1)
                    dve.wait_ge(zd_filled, c + 1)
                    dve.tensor_copy(zcar[:, :], zd[s][:, C - 1, :]).then_inc(zcar_saved, 1)
                    dve.wait_ge(zcar_saved, c + 1)
                    dve.wait_ge(zs_gathered[s], 16 * C * (i + 1))
                    dve.tensor_tensor(zd[s], zd[s], zs[s], ALU.mult).then_inc(product_done, 1)
                    dve.wait_ge(product_done, c + 1)
                    dve.tensor_reduce(logit[:, :, :].rearrange("p h c -> p c h"),
                                      zd[s].rearrange("p c (h r) -> p c h r", r=R), AX_X, ALU.add
                                      ).then_inc(zd_used[s], 1)
                    dve.wait_ge(zd_used[s], i + 1)
                    dve.wait_ge(kneg_done, c + 1)
                    dve.wait_ge(mcar_done, c + 1)
                    wait(dve, max_stored, c)
                    for h in range(H):
                        ins = dve.tensor_tensor_scan(mx[s][:, h, 1:C + 1], kneg[:, :], logit[:, h, :],
                                                     mx[s][:, h, 0:1], ALU.add, ALU.max)
                    ins.then_inc(max_done, 1)
                    dve.wait_ge(max_done, c + 1)
                    dve.tensor_tensor(ex[:, 0, :, :], mx[s][:, :, 0:C],
                                      kneg[:, :].unsqueeze(1).broadcast_to([P, H, C]), ALU.add).then_inc(restart_added, 1)
                    dve.tensor_tensor(ex[:, 1, :, :], logit[:, :, :], mx[s][:, :, 1:C + 1], ALU.subtract
                                      ).then_inc(diff_done, 1)
                    dve.wait_ge(restart_added, c + 1)
                    dve.tensor_tensor(ex[:, 0, :, :], ex[:, 0, :, :], mx[s][:, :, 1:C + 1], ALU.subtract
                                      ).then_inc(diff_done, 1)
                    dve.wait_ge(exp_done, c + 1)
                    wide = ex[:, 1, :, :].rearrange("p h c -> p c h").unsqueeze(3).broadcast_to([P, C, H, R])
                    zs4 = zs[s].rearrange("p c (h r) -> p c h r", r=R)
                    dve.tensor_tensor(zs4, zs4, wide, ALU.mult).then_inc(weighted, 1)
                    wait(dve, scar_saved, c)
                    dve.tensor_tensor(zhead[:, :].rearrange("p (h r) -> p h r", r=R),
                                      scar[:, 0:F].rearrange("p (h r) -> p h r", r=R),
                                      ex[:, 0, :, 0:1].broadcast_to([P, H, R]), ALU.mult).then_inc(head_made, 1)
                    wait(dve, rows0_stored[s], 16 * i)
                    for h in range(H):
                        dve.tensor_tensor_scan(row0[s][:, :, F + h], ex[:, 0, h, :], ex[:, 1, h, :],
                                               scar[:, F + h:F + h + 1], ALU.mult, ALU.add)
                    dve.wait_ge(weighted, c + 1)
                    dve.wait_ge(head_made, c + 1)
                    dve.tensor_tensor(zs[s][:, 0, :], zs[s][:, 0, :], zhead[:, :], ALU.add).then_inc(sums_begun, 1)
                    dve.wait_ge(sums_begun, c + 1)
                    for f in range(F):
                        ins = dve.tensor_tensor_scan(row0[s][:, :, f], ex[:, 0, f // R, :], zs[s][:, :, f],
                                                     0.0, ALU.mult, ALU.add)
                    ins.then_inc(sums_done[s], 1)
                    dve.wait_ge(sums_done[s], i + 1)
                    dve.tensor_copy(scar[:, :], row0[s][:, C - 1, 0:F + H]).then_inc(scar_saved, 1)

            rounds(dve, NCH // 2, edge_chunks)

            m = [0]

            def mend(ins, read_next=True):
                m[0] += 1
                ins.then_inc(mend_dve, 1)
                if read_next:
                    dve.wait_ge(mend_dve, m[0])

            lastrow = row0[1][:, C - 1, :]
            wideS = scratch[:, 512:512 + 4 * F].rearrange("p (k f) -> p k f", f=F)
            mend(dve.memset(got[:, :], 0.0), read_next=False)
            dve.wait_ge(scar_saved, NCH)
            dve.wait_ge(max_stored, NCH)

            def over_heads(ap):
                return ap.unsqueeze(2).broadcast_to([P, H, R])

            mend(dve.tensor_copy(wideS[:, 0, :], lastrow[:, 0:F]), read_next=False)
            mend(dve.tensor_copy(wideS[:, 1, :].rearrange("p (h r) -> p h r", r=R), over_heads(lastrow[:, F:F + H])),
                 read_next=False)
            mend(dve.tensor_copy(wideS[:, 2, :].rearrange("p (h r) -> p h r", r=R),
                                 over_heads(lastrow[:, F + H:ROW])), read_next=False)
            mend(dve.tensor_copy(wideS[:, 3, :], keep_all[:, 0:1].broadcast_to([P, F])), read_next=False)
            dve.wait_ge(mend_pe, 1)
            tr = T[0][0:F, :].rearrange("f (k p) -> f k p", p=P)
            carry = scratch[0:F, 1024:1024 + 3 * (P + 1)].rearrange("f (k p) -> f k p", p=P + 1)
            negk = scratch[0:F, 512:512 + P]
            dve.memset(carry[:, 0:2, 0:1], 0.0)
            dve.memset(carry[:, 2, 0:1], LOWEST)
            mend(dve.tensor_scalar(negk, tr[:, 3, :], -1.0, -LOWEST, ALU.add, ALU.mult))
            mend(dve.tensor_tensor_scan(carry[:, 2, 1:P + 1], negk, tr[:, 2, :], LOWEST, ALU.add, ALU.max))
            done(dve.tensor_tensor(negk, carry[:, 2, 0:P], negk, ALU.add))
            dve.tensor_tensor(negk, negk, carry[:, 2, 1:P + 1], ALU.subtract)
            mend(dve.tensor_tensor(scratch[0:F, 512 + P:512 + 2 * P], tr[:, 2, :], carry[:, 2, 1:P + 1],
                                   ALU.subtract))
            dve.wait_ge(mend_act, 1)
            both = scratch[0:F, 512 + 2 * P:512 + 4 * P].rearrange("f (k p) -> f k p", p=P)
            mend(dve.tensor_tensor(both, tr[:, 0:2, :],
                                   scratch[0:F, 512 + P:512 + 2 * P].unsqueeze(1).broadcast_to([F, 2, P]), ALU.mult))
            dve.tensor_tensor_scan(carry[:, 0, 1:P + 1], scratch[0:F, 512:512 + P], both[:, 0, :], 0.0,
                                   ALU.mult, ALU.add)
            mend(dve.tensor_tensor_scan(carry[:, 1, 1:P + 1], scratch[0:F, 512:512 + P], both[:, 1, :], 0.0,
                                        ALU.mult, ALU.add))
            dve.wait_ge(mend_pe, 2)
            dve.wait_ge(mend_dma, 16)
            cr = T[1][:, 0:3 * F].rearrange("p (k f) -> p k f", f=F)
            wideR = scratch[:, 512 + 3 * F:512 + 6 * F].rearrange("p (k f) -> p k f", f=F)
            dve.tensor_copy(wideR[:, 0, :].rearrange("p (h r) -> p h r", r=R), over_heads(got[:, F:F + H]))
            mend(dve.tensor_copy(wideR[:, 1, :].rearrange("p (h r) -> p h r", r=R), over_heads(got[:, F + H:ROW])))
            mend(dve.tensor_tensor(wideR[:, 2, :], cr[:, 2, :], wideR[:, 1, :], ALU.max))
            dve.tensor_tensor(scratch[:, 512:512 + F], cr[:, 2, :], wideR[:, 2, :], ALU.subtract)
            mend(dve.tensor_tensor(scratch[:, 512 + F:512 + 2 * F], wideR[:, 1, :], wideR[:, 2, :], ALU.subtract))
            dve.wait_ge(mend_act, 2)
            ea = scratch[:, 512:512 + F]
            eb = scratch[:, 512 + F:512 + 2 * F]
            part1 = scratch[:, 512 + 6 * F:512 + 7 * F]
            part2 = scratch[:, 512 + 7 * F:512 + 8 * F]
            dve.tensor_tensor(part1, cr[:, 0, :], ea, ALU.mult)
            dve.tensor_tensor(part2, cr[:, 1, :], ea, ALU.mult)
            dve.tensor_tensor(got[:, 0:F], got[:, 0:F], eb, ALU.mult)
            done(dve.tensor_tensor(wideR[:, 0, :], wideR[:, 0, :], eb, ALU.mult))
            heads = [w.rearrange("p (h r) -> p h r", r=R)[:, :, 0] for w in (part2, wideR[:, 0, :], wideR[:, 2, :])]
            mend(dve.tensor_tensor(got[:, 0:F], got[:, 0:F], part1, ALU.add))
            dve.tensor_tensor(got[:, F:F + H], heads[0], heads[1], ALU.add)
            mend(dve.tensor_copy(got[:, F + H:ROW], heads[2]))
            assert m[0] == DA, m[0]

            def first_indices(layer):
                for s in range(2):
                    dve.tensor_copy(nidx[s][:, :], last_i[:, s * GB:(s + 1) * GB]).then_inc(n_idx[layer], 1)

            def next_indices(layer, i, s):
                dve.wait_ge(n_gathered[layer][s], 16 * GB * (i + 1))
                dve.tensor_copy(nidx[s][:, :], last_i[:, bass.ds((2 * i + s + 2) * GB, GB)]
                                ).then_inc(n_idx[layer], 1)

            def scale(i, s):
                g = 2 * i + s
                next_indices(0, i, s)
                wait(dve, n_scaled, g)
                dve.tensor_scalar(rec[:, :, :], ng0[s][:, :, F:F + H], 1e-16, None, ALU.add).then_inc(agg_step, 1)
                dve.wait_ge(agg_step, 3 * g + 1)
                dve.reciprocal(rec[:, :, :], rec[:, :, :]).then_inc(agg_step, 1)
                dve.wait_ge(agg_step, 3 * g + 2)
                dve.tensor_tensor(rec[:, :, :], rec[:, :, :],
                                  filled[:, bass.ds(g * GB, GB)].unsqueeze(2).broadcast_to([P, GB, H]), ALU.mult
                                  ).then_inc(agg_step, 1)
                dve.wait_ge(agg_step, 3 * g + 3)
                wait(dve, n_turned[0], NQ * (g - 1))
                dve.tensor_tensor(aggn[s].rearrange("p b (h r) -> p b h r", r=R),
                                  ng0[s][:, :, 0:F].rearrange("p b (h r) -> p b h r", r=R),
                                  rec[:, :, :].unsqueeze(3).broadcast_to([P, GB, H, R]), ALU.mult
                                  ).then_inc(n_scaled, 1)

            def finish_stats(layer, i, s):
                dve.wait_ge(n_std[layer], 2 * i + s + 1)
                dve.reciprocal(rstd[s][:, :], rstd[s][:, :]).then_inc(n_inv[layer], 1)
                dve.wait_ge(n_inv[layer], 2 * i + s + 1)
                dve.scalar_tensor_tensor(out=shiftm[s][:, :], in0=mv[s][:, :, 0], scalar=-1.0, in1=rstd[s][:, :],
                                         op0=ALU.mult, op1=ALU.mult).then_inc(n_rstd[layer], 1)

            def combine(layer, i, s):
                g = 2 * i + s
                before = (i, 0) if s else (i - 1, 1)
                there = not (isinstance(i, int) and i == 0 and s == 0)
                dve.wait_ge(n_loaded[layer][s], 48 * (i + 1))
                wait(dve, n_normed[layer], g - 1)
                for q in range(NQ + 1):
                    if q < NQ:
                        dve.wait_ge(n_made[layer], NQ * g + q + 1)
                        pair = slice(2 * q, 2 * q + len(PAIRS[q]))
                        if layer == 0:
                            dve.tensor_tensor(hg[s][:, pair, :], O_of[q][:, 0:len(PAIRS[q]), :],
                                              xg[s][:, pair, :], ALU.max).then_inc(n_taken[0], 1)
                        else:
                            for j, b in enumerate(PAIRS[q]):
                                ins = dve.scalar_tensor_tensor(out=yg[s][:, b, :], in0=O_of[q][:, j, :],
                                                               scalar=inv[:, bass.ds(g * GB + b, 1)],
                                                               in1=yg[s][:, b, :], op0=ALU.mult, op1=ALU.add)
                            ins.then_inc(n_taken[1], 1)
                            dve.wait_ge(n_taken[1], NQ * g + q + 1)
                            dve.scalar_tensor_tensor(out=hg[s][:, pair, :], in0=xg[s][:, pair, :], scalar=2.0,
                                                     in1=yg[s][:, pair, :], op0=ALU.mult, op1=ALU.max
                                                     ).then_inc(n_summed[1], 1)
                    if q == 1 and there:
                        finish_stats(layer, *before)
                    if q > 0:
                        dve.wait_ge(n_taken[0] if layer == 0 else n_summed[1], NQ * g + q)
                        for b in PAIRS[q - 1]:
                            dve.bn_stats(stats[s][:, b, :], hg[s][:, b, :]).then_inc(n_stats[layer], 1)
                dve.wait_ge(n_stats[layer], GB * (g + 1))
                if layer == 0:
                    dve.sem_inc(n_summed[0], NQ)
                else:
                    dve.sem_inc(gate, 1)
                for b in range(GB):
                    dve.bn_aggr(mv[s][:, b, :], stats[s][:, b, :]).then_inc(n_mv[layer], 1)

            first_indices(0)
            scale(0, 0)
            scale(0, 1)
            combine(0, 0, 0)
            with dve.Fori(1, NG // 2) as i:
                scale(i, 0)
                combine(0, i - 1, 1)
                scale(i, 1)
                combine(0, i, 0)
            combine(0, NG // 2 - 1, 1)
            finish_stats(0, NG // 2 - 1, 1)

            car = scratch[:, 512:512 + D]
            dve.memset(car, 0.0).then_inc(car1_saved, 1)
            for s in range(S1):
                dve.tensor_copy(idx[s][:, :], src_i[:, s * C:(s + 1) * C]).then_inc(idx1_ready[s], 1)

            def sum_rows(i, s):
                c = S1 * i + s
                wait(dve, col_summed, c * C)
                dve.tensor_copy(keepc[:, :], keep[:, bass.ds(c * C, C)]).then_inc(keepc_made, 1)
                dve.wait_ge(keepc_made, c + 1)
                for j in range(C):
                    if j == 0:
                        dve.wait_ge(r_gathered[0][s], 16 * CA * (i + 1))
                        dve.wait_ge(car1_saved, c + 1)
                    elif j == CA:
                        dve.wait_ge(r_gathered[1][s], 16 * (C - CA) * (i + 1))
                    if j > 0:
                        dve.wait_ge(col_summed, c * C + j)
                    before = car if j == 0 else slot1[s][:, j - 1, :]
                    dve.scalar_tensor_tensor(out=slot1[s][:, j, :], in0=before, scalar=keepc[:, j:j + 1],
                                             in1=slot1[s][:, j, :], op0=ALU.mult, op1=ALU.add
                                             ).then_inc(col_summed, 1)
                dve.tensor_copy(idx[s][:, :], src_i[:, bass.ds((c + S1) * C, C)]).then_inc(idx1_ready[s], 1)
                dve.wait_ge(col_summed, (c + 1) * C)
                dve.tensor_copy(car, slot1[s][:, C - 1, :]).then_inc(car1_saved, 1)

            rounds(dve, NCH // S1, lambda i: [sum_rows(i, s) for s in range(S1)])
            for s in range(NCH % S1):
                sum_rows(NCH // S1, s)

            mend(dve.memset(got[:, :], 0.0))
            dve.wait_ge(car1_saved, NCH + 1)
            mend(dve.tensor_copy(scratch[:, 512 + D:512 + D + P], keep_all[:, 0:1].broadcast_to([P, P])))
            carry1 = scratch[:, 1024:1024 + 2 * (P + 1)].rearrange("f (k p) -> f k p", p=P + 1)
            mend(dve.memset(carry1[:, :, 0:1], 0.0))
            dve.wait_ge(mend_pe, 3)
            keepT = scratch[:, 512 + D + P:512 + D + 2 * P]
            mend(dve.tensor_copy(keepT, T[0][:, KD * P:(KD + 1) * P]))
            for k in range(KD):
                mend(dve.tensor_tensor_scan(carry1[:, k, 1:P + 1], keepT, T[0][:, k * P:(k + 1) * P], 0.0,
                                            ALU.mult, ALU.add))
            dve.sem_inc(mend_dve, 1)
            m[0] += 1
            dve.wait_ge(mend_pe, 4)
            dve.wait_ge(mend_dma, 48)
            mend(dve.tensor_tensor(got[:, :], got[:, :], T[1][:, 0:D], ALU.add))
            dve.sem_inc(mend_dve, 1)
            assert m[0] == DA + 8, m[0]

            first_indices(1)
            next_indices(1, 0, 0)
            next_indices(1, 0, 1)
            combine(1, 0, 0)
            with dve.Fori(1, NG // 2 - 1) as i:
                next_indices(1, i, 0)
                combine(1, i - 1, 1)
                next_indices(1, i, 1)
                combine(1, i, 0)
            combine(1, NG // 2 - 2, 1)
            combine(1, NG // 2 - 1, 0)
            combine(1, NG // 2 - 1, 1)
            finish_stats(1, NG // 2 - 1, 1)


_INS = ['x', 'src', 'dst', 'L0_gnn_U', 'L0_gnn_Dmat', 'L0_gnn_head_w', 'L1_gnn_W_l', 'L1_gnn_b_l', 'L1_gnn_W_r']


def kernel(**inputs):
    import numpy as _np
    import concourse.bacc as _bacc
    from concourse import mybir as _mybir
    from concourse.bass_utils import run_bass_kernel_spmd as _run

    nc = _bacc.Bacc("TRN2", target_bir_lowering=False, num_devices=1,
                      dynamic_dma_scratch_size=8192)
    arrays, args = {}, []
    for name in _INS:
        a = _np.ascontiguousarray(inputs[name])
        arrays[f"in_{name}_dram"] = a
        args.append(nc.dram_tensor(f"in_{name}_dram", a.shape, _mybir.dt.from_np(a.dtype), kind="ExternalInput").ap())
    args.append(nc.dram_tensor("out_dram", inputs["x"].shape, _mybir.dt.float32, kind="ExternalOutput").ap())
    gnn_kernel(nc, *args)
    r = _run(nc, [arrays], core_ids=[0])
    return r.results[0]["out_dram"]
```
